# Optimizing a Trainium2 kernel written in Bass

```python
import numpy as np
import jax
import jax.numpy as jnp

def _softmax(x, axis=-1):
    return jax.nn.softmax(x, axis=axis)

def _gelu(x):
    return jax.nn.gelu(x, approximate=True)

def _silu(x):
    return jax.nn.silu(x)

def _sigmoid(x):
    return jax.nn.sigmoid(x)

def _layernorm(x, axis=-1, eps=1e-05):
    m = jnp.mean(x, axis=axis, keepdims=True)
    v = jnp.var(x, axis=axis, keepdims=True)
    return (x - m) / jnp.sqrt(v + eps)

def _scatter_add(tgt, idx, src, axis=0):
    return tgt.at[idx].add(src)

def _segment_sum(src, seg, n):
    return jax.ops.segment_sum(src, seg, n)
kernel_name = 'mk_adaln_ffn_d2_seqx_r4_0d8ace'

def setup_inputs(seed: int=0):
    np.random.seed(seed)
    _w = jnp.asarray

    def _rec_inputs():
        import jax
        import jax.numpy as jnp
        _rk = jax.random.key(seed)
        x = -7.109e-05 + 0.9999 * jax.random.normal(jax.random.fold_in(_rk, 1), (128, 64, 1024), jnp.float32)
        _lenS = 64 - jax.random.randint(jax.random.fold_in(_rk, 7), (128,), 0, max(1, 64 // 4) + 1, jnp.int32)
        _lenS2 = 64 - jax.random.randint(jax.random.fold_in(_rk, 8), (128,), 0, max(1, 64 // 4) + 1, jnp.int32)
        itok_B_0_15 = jax.random.randint(jax.random.fold_in(_rk, 11), (128,), 0, 16, jnp.int32)
        itok_B_6_15 = jax.random.randint(jax.random.fold_in(_rk, 12), (128,), 6, 16, jnp.int32)
        return (x, itok_B_0_15, itok_B_6_15)
    x, itok_B_0_15, itok_B_6_15 = _rec_inputs()

    def _L0_cond_setup():
        import jax, jax.numpy as jnp
        import numpy as np
        NUM_CONDITIONS = 16
        IN_CH = 64
        OUT_CH = 64
        B = 64
        T = 1024
        key = jax.random.key(seed)
        k_x, k_w, k_c = jax.random.split(key, 3)
        x = jax.random.normal(k_x, (B, IN_CH, T), dtype=jnp.float32)
        bound = float(np.sqrt(6.0 / IN_CH))
        weights = jax.random.uniform(k_w, (NUM_CONDITIONS, IN_CH, OUT_CH), dtype=jnp.float32, minval=-bound, maxval=bound)
        condition = jax.random.randint(k_c, (B,), 0, NUM_CONDITIONS, dtype=jnp.int64)
        return {'x': x, 'weights': weights, 'condition': condition}
    _L0_cond_all = _L0_cond_setup()
    _L0_cond_in = {k: v for k, v in _L0_cond_all.items() if k in ('weights',)}
    del _L0_cond_all

    def _L0_ffn_setup():
        import jax, jax.numpy as jnp
        import numpy as np
        R = 16
        NUM_EXPERTS = 8
        TOP_K = 2
        LORA_ALPHA = 32
        SCALING = LORA_ALPHA / R
        key = jax.random.key(seed)
        ks = jax.random.split(key, 6)
        d_in, d_out = (1024, 1024)
        x = jax.random.normal(ks[0], (4, 512, d_in), dtype=jnp.float32)
        W_base = jax.random.normal(ks[1], (d_out, d_in), dtype=jnp.float32) * 0.02
        b_base = jax.random.normal(ks[2], (d_out,), dtype=jnp.float32) * 0.02
        W_router = jax.random.normal(ks[3], (NUM_EXPERTS, d_in), dtype=jnp.float32) * 0.01
        A = jax.random.normal(ks[4], (NUM_EXPERTS, R, d_in), dtype=jnp.float32) * 0.02
        B = jax.random.normal(ks[5], (NUM_EXPERTS, d_out, R), dtype=jnp.float32) * 0.02
        return {'x': x, 'W_base': W_base, 'b_base': b_base, 'W_router': W_router, 'A': A, 'B': B}
    _L0_ffn_all = _L0_ffn_setup()
    _L0_ffn_in = {k: v for k, v in _L0_ffn_all.items() if k in ('W_base', 'b_base', 'W_router', 'A', 'B')}
    del _L0_ffn_all

    def _L1_cond_setup():
        import jax, jax.numpy as jnp
        import numpy as np
        B, S, D_IN, D_OUT = (4, 512, 1024, 1024)
        RANK, MAX_LORAS = (16, 32)
        key = jax.random.key(seed)
        ks = jax.random.split(key, 6)
        x = jax.random.normal(ks[0], (B, S, D_IN), dtype=jnp.float32)
        adapter_ids = jax.random.randint(ks[1], (B,), 0, MAX_LORAS)
        base_weight = jax.random.normal(ks[2], (D_OUT, D_IN), dtype=jnp.float32) * D_IN ** (-0.5)
        base_bias = jax.random.normal(ks[3], (D_OUT,), dtype=jnp.float32) * 0.01
        lora_A_w = jax.random.normal(ks[4], (MAX_LORAS, RANK, D_IN), dtype=jnp.float32) * D_IN ** (-0.5)
        lora_B_w = jax.random.normal(ks[5], (MAX_LORAS, D_OUT, RANK), dtype=jnp.float32) * RANK ** (-0.5)
        return {'x': x, 'adapter_ids': adapter_ids, 'base_weight': base_weight, 'base_bias': base_bias, 'lora_A_w': lora_A_w, 'lora_B_w': lora_B_w}
    _L1_cond_all = _L1_cond_setup()
    _L1_cond_in = {k: v for k, v in _L1_cond_all.items() if k in ('base_weight', 'base_bias', 'lora_A_w', 'lora_B_w')}
    del _L1_cond_all

    def _L1_ffn_setup():
        import jax, jax.numpy as jnp
        import numpy as np
        FP8 = jnp.float8_e4m3fn

        def _quant_fp8(x, scale_inv):
            return (x * scale_inv).astype(FP8)
        key = jax.random.key(seed)
        k1, k2, k3 = jax.random.split(key, 3)
        B, S, IN, OUT = (4, 512, 1024, 1024)
        inp = jax.random.normal(k1, (B, S, IN), dtype=jnp.float32)
        weight = jax.random.normal(k2, (IN, OUT), dtype=jnp.float32) * 0.02
        bias = jax.random.normal(k3, (OUT,), dtype=jnp.float32)
        input_scale = jnp.ones((1,), dtype=jnp.float32)
        weight_scale = jnp.ones((1,), dtype=jnp.float32)
        return {'inp': inp, 'weight': weight, 'bias': bias, 'input_scale': input_scale, 'weight_scale': weight_scale}
    _L1_ffn_all = _L1_ffn_setup()
    _L1_ffn_in = {k: v for k, v in _L1_ffn_all.items() if k in ('weight', 'bias', 'input_scale', 'weight_scale')}
    del _L1_ffn_all
    return {'x': x, 'itok_B_0_15': itok_B_0_15, 'itok_B_6_15': itok_B_6_15, 'L0_cond_weights': _L0_cond_in['weights'], 'L0_ffn_W_base': _L0_ffn_in['W_base'], 'L0_ffn_b_base': _L0_ffn_in['b_base'], 'L0_ffn_W_router': _L0_ffn_in['W_router'], 'L0_ffn_A': _L0_ffn_in['A'], 'L0_ffn_B': _L0_ffn_in['B'], 'L1_cond_base_weight': _L1_cond_in['base_weight'], 'L1_cond_base_bias': _L1_cond_in['base_bias'], 'L1_cond_lora_A_w': _L1_cond_in['lora_A_w'], 'L1_cond_lora_B_w': _L1_cond_in['lora_B_w'], 'L1_ffn_weight': _L1_ffn_in['weight'], 'L1_ffn_bias': _L1_ffn_in['bias'], 'L1_ffn_input_scale': _L1_ffn_in['input_scale'], 'L1_ffn_weight_scale': _L1_ffn_in['weight_scale']}

def reference(x, itok_B_0_15, itok_B_6_15, L0_cond_weights, L0_ffn_W_base, L0_ffn_b_base, L0_ffn_W_router, L0_ffn_A, L0_ffn_B, L1_cond_base_weight, L1_cond_base_bias, L1_cond_lora_A_w, L1_cond_lora_B_w, L1_ffn_weight, L1_ffn_bias, L1_ffn_input_scale, L1_ffn_weight_scale):
    import jax
    import jax.numpy as jnp

    def _L0_cond_ref(x, weights, condition):
        import jax, jax.numpy as jnp
        import numpy as np
        NUM_CONDITIONS = 16
        IN_CH = 64
        OUT_CH = 64
        B = 64
        T = 1024
        W = weights[condition]
        return jnp.einsum('bct,bcd->bdt', x, W)

    def _L0_ffn_ref(x, W_base, b_base, W_router, A, B):
        import jax, jax.numpy as jnp
        import numpy as np
        R = 16
        NUM_EXPERTS = 8
        TOP_K = 2
        LORA_ALPHA = 32
        SCALING = LORA_ALPHA / R
        orig_shape = x.shape
        d_in = x.shape[-1]
        x_flat = x.reshape(-1, d_in)
        logits = x_flat @ W_router.T
        probs = jax.nn.softmax(logits, axis=-1)
        topk_probs, topk_idx = jax.lax.top_k(probs, TOP_K)
        topk_probs = topk_probs / jnp.sum(topk_probs, axis=-1, keepdims=True)
        onehot = jax.nn.one_hot(topk_idx, NUM_EXPERTS, dtype=x.dtype)
        combine = jnp.einsum('nk,nke->ne', topk_probs, onehot)
        h = jnp.einsum('nd,erd->ner', x_flat, A)
        hw = h * combine[:, :, None]
        expert_out = jnp.einsum('ner,eor->no', hw, B) * SCALING
        base_out = x_flat @ W_base.T + b_base
        out = base_out + expert_out
        return out.reshape(*orig_shape[:-1], W_base.shape[0])

    def _L1_cond_ref(x, adapter_ids, base_weight, base_bias, lora_A_w, lora_B_w):
        import jax, jax.numpy as jnp
        import numpy as np
        B, S, D_IN, D_OUT = (4, 512, 1024, 1024)
        RANK, MAX_LORAS = (16, 32)
        result = jnp.einsum('bsd,od->bso', x, base_weight) + base_bias
        A = lora_A_w[adapter_ids]
        Bw = lora_B_w[adapter_ids]
        h = jnp.einsum('bsd,brd->bsr', x, A)
        lora_out = jnp.einsum('bsr,bor->bso', h, Bw)
        result = result + lora_out
        return result.astype(x.dtype)

    def _L1_ffn_ref(inp, weight, bias, input_scale, weight_scale):
        import jax, jax.numpy as jnp
        import numpy as np
        FP8 = jnp.float8_e4m3fn

        def _quant_fp8(x, scale_inv):
            return (x * scale_inv).astype(FP8)
        in_features = weight.shape[0]
        lead = inp.shape[:-1]
        x = inp.reshape(-1, in_features)
        x_q = _quant_fp8(x, 1.0 / input_scale)
        w_q = _quant_fp8(weight, 1.0 / weight_scale)
        acc = jnp.einsum('ni,io->no', x_q.astype(jnp.float32), w_q.astype(jnp.float32))
        out = acc * (input_scale * weight_scale) + bias
        return out.reshape(*lead, out.shape[-1])
    x = x + _L0_ffn_ref(_L0_cond_ref(x, L0_cond_weights, itok_B_0_15), L0_ffn_W_base, L0_ffn_b_base, L0_ffn_W_router, L0_ffn_A, L0_ffn_B)
    x = x + _L1_ffn_ref(_L1_cond_ref(x, itok_B_6_15, L1_cond_base_weight, L1_cond_base_bias, L1_cond_lora_A_w, L1_cond_lora_B_w), L1_ffn_weight, L1_ffn_bias, L1_ffn_input_scale, L1_ffn_weight_scale)
    return x

_drawn_inputs = setup_inputs


def setup_inputs(seed=0):
    import zlib

    import numpy as np

    out = dict(_drawn_inputs(seed))
    spreads = {}
    factors = {'L0_ffn_b_base': 3.122, 'L1_cond_base_bias': 6.932}
    for name, (base, spread) in spreads.items():
        noise = np.random.default_rng([zlib.crc32(name.encode()), seed]).standard_normal(out[name].shape)
        drawn = base * np.exp(spread * noise) if base else spread * noise
        out[name] = jnp.asarray(drawn.astype(out[name].dtype))
    for name, factor in factors.items():
        out[name] = (out[name] * factor).astype(out[name].dtype)
    return out
```

```python
from contextlib import ExitStack

import numpy as np

import concourse.bass as bass
from concourse import mybir

F32 = mybir.dt.float32
F32R = mybir.dt.float32r
BF16 = mybir.dt.bfloat16
U32 = mybir.dt.uint32
I32 = mybir.dt.int32
ALU = mybir.AluOpType
ACT = mybir.ActivationFunctionType
AXIS = mybir.AxisListType

P = 128
BATCH, CH, D = 128, 64, 1024
TILES = BATCH * CH // P
PER_TILE = P // CH
KC = D // P
HALF = 512
EXPERTS, RANK = 8, 16
ER = EXPERTS * RANK
LORA_SCALE = 2.0
LORAS = 32
LR = PER_TILE * RANK

G0_START = (0, 392, 776)
G0_WIDTH = (392, 384, 384)
G0_OUT = (ER + EXPERTS, 0, 0)
G0_COL = (0, 256, 640)
W0_COLS = ER + EXPERTS + D

G1_BASE = (320, 352, 352)
G1_COL = (0, 320, 672)
G1_AT = (LR, 2 * LR + 320, 2 * LR + 320 + 352)
W1_COLS = 2 * LR + D
STACK = 3 * LR + 2

ROUND_C = 1.5 * 2.0 ** 20
MIN_NORMAL = 2.0 ** -6
OVERFLOW_C = float(np.float32(2.0 ** 127 / 235.0))

WQ_TILES = range(2, 10)
POOL_UNITS_A_TILE = 3


def build(nc, x, ids0, ids1, wc, m0, b0, b_base, w1t, base_bias, a1, b1, wf, bias2, s_in, s_w, out):
    x_t = x.rearrange("b c t -> (b c) t").rearrange("(n p) t -> n p t", p=P)
    out_t = out.rearrange("b c t -> (b c) t").rearrange("(n p) t -> n p t", p=P)
    x1_dram = nc.dram_tensor("x1_scratch", (TILES, P, D), F32, kind="Internal").ap()
    a1_dram = nc.dram_tensor("a1_split", (LORAS, P, 2 * KC * RANK), F32, kind="Internal").ap()
    b1_dram = nc.dram_tensor("b1_split", (LORAS * RANK, 2, D), F32, kind="Internal").ap()
    b1_ids = b1_dram.rearrange("(i r) s n -> i r s n", r=RANK)

    with ExitStack() as whole:
        def sb(name, shape, dt, stack=whole):
            return stack.enter_context(nc.sbuf_tensor(name, shape, dt))

        def sem(name):
            return whole.enter_context(nc.semaphore(name))

        bank_g = whole.enter_context(nc.psum_tensor("bank_g", [P, 3, 512], F32))
        bank_t = whole.enter_context(nc.psum_tensor("bank_t", [P, 2, 512], F32))
        bank_f = whole.enter_context(nc.psum_tensor("bank_f", [P, 2, 512], F32))
        bank_m = whole.enter_context(nc.psum_tensor("bank_m", [P, 512], F32))
        rq_ps = bank_m[:, :].bitcast(BF16)

        w1h = sb("w1h", [P, KC * W1_COLS], F32R)
        w1l = sb("w1l", [P, KC * W1_COLS], F32R)
        w1h_k = w1h[:, :].rearrange("p (k n) -> p k n", k=KC)
        w1l_k = w1l[:, :].rearrange("p (k n) -> p k n", k=KC)
        wq = sb("wq", [P, KC, D], BF16)
        ident = sb("ident", [P, P], F32)
        ident_b = sb("ident_b", [P, P], BF16)
        slot_mask = sb("slot_mask", [P, LR], F32)
        ids0_sb = sb("ids0_sb", [1, BATCH], I32)
        ids1_sb = sb("ids1_sb", [1, BATCH], I32)
        s_in_sb = sb("s_in_sb", [P, 1], F32)
        s_w_sb = sb("s_w_sb", [P, 1], F32)
        inv_in = sb("inv_in", [P, 1], F32)
        inv_w = sb("inv_w", [P, 1], F32)
        s_out = sb("s_out", [P, 1], F32)

        s_ids = sem("s_ids")
        s_const = sem("s_const")
        s_ident = sem("s_ident")
        mask_set = sem("mask_set")
        s_scale = sem("s_scale")

        with ExitStack() as p1:
            w0h = sb("w0h", [P, KC, W0_COLS], F32R, p1)
            w0l = sb("w0l", [P, KC, W0_COLS], F32R, p1)
            b0h = sb("b0h", [P, D], F32R, p1)
            b0l = sb("b0l", [P, D], F32R, p1)
            xbuf = sb("xbuf", [P, 2, D], F32, p1)
            x1buf = sb("x1buf", [P, 2, D], F32, p1)
            yh = sb("yh", [P, D], F32R, p1)
            yl = sb("yl", [P, D], F32R, p1)
            wbd = sb("wbd", [P, 2, P], F32, p1)
            b_base_sb = sb("b_base_sb", [P, D], F32, p1)
            hw = sb("hw", [P, ER], F32, p1)
            hwt_h = sb("hwt_h", [P, P], F32R, p1)
            hwt_l = sb("hwt_l", [P, P], F32R, p1)
            pool_raw = sb("pool_raw", [P, 2, HALF], F32, p1)
            wq_val = sb("wq_val", [P, 2, HALF], F32, p1)
            wq_pow = sb("wq_pow", [P, HALF], F32, p1)
            wq_nan = wq_pow[:, :].bitcast(BF16)[:, 0:HALF]
            negmax = sb("negmax", [P, 1], F32, p1)
            esum = sb("esum", [P, 1], F32, p1)
            rsum = sb("rsum", [P, 1], F32, p1)
            top_sum = sb("top_sum", [P, 1], F32, p1)
            top_inv = sb("top_inv", [P, 1], F32, p1)
            expo = sb("expo", [P, EXPERTS], F32, p1)
            probs = sb("probs", [P, 2 * EXPERTS], F32, p1)
            sorted8 = sb("sorted8", [P, 8], F32, p1)
            to_replace = sb("to_replace", [P, 8], F32, p1)
            without_top = sb("without_top", [P, 2 * EXPERTS], F32, p1)
            top_probs = sb("top_probs", [P, EXPERTS], F32, p1)

            stage = [x1buf[:, q // 2, (q % 2) * HALF:(q % 2 + 1) * HALF] for q in range(4)]

            x_loaded = [sem(f"x_loaded{b}") for b in range(2)]
            wc_loaded = [sem(f"wc_loaded{b}") for b in range(2)]
            stage_loaded = [sem(f"stage_loaded{q}") for q in range(4)]
            w0_hi = sem("w0_hi")
            w0_lo = sem("w0_lo")
            bias_loaded = sem("bias_loaded")
            wbd_zeroed = sem("wbd_zeroed")
            y_ps = [sem(f"y_ps{h}") for h in range(2)]
            yh_done = [sem(f"yh_done{h}") for h in range(2)]
            yl_done = [sem(f"yl_done{h}") for h in range(2)]
            h_ps = sem("h_ps")
            negmax_done = sem("negmax_done")
            exp_done = sem("exp_done")
            rsum_done = sem("rsum_done")
            probs_done = sem("probs_done")
            sorted_done = sem("sorted_done")
            replace_done = sem("replace_done")
            top_sum_done = sem("top_sum_done")
            top_inv_done = sem("top_inv_done")
            without_done = sem("without_done")
            top_done = sem("top_done")
            hw_done = sem("hw_done")
            hwt_ps = sem("hwt_ps")
            hwth_done = sem("hwth_done")
            hwtl_done = sem("hwtl_done")
            acc_ps = [sem(f"acc_ps{g}") for g in range(3)]
            xb_done = sem("xb_done")
            x1_done = [sem(f"x1_done{g}") for g in range(3)]
            x1_stored = [sem(f"x1_stored{b}") for b in range(2)]
            pool_loaded = [sem(f"pool_loaded{b}") for b in range(2)]
            pool_hi = sem("pool_hi")
            pool_lo = sem("pool_lo")
            split_stored = sem("split_stored")
            wq_loaded = [sem(f"wq_loaded{b}") for b in range(2)]
            wq_step = sem("wq_step")

            w0_units = [("w", g, k) for g in range(2) for k in range(KC)]
            w0_units += [("b", h, 0) for h in range(2)]
            w0_units += [("w", 2, k) for k in range(KC)]
            w0_need = (KC, 2 * KC, len(w0_units))

            def w0_places(unit):
                kind, g, k = unit
                if kind == "b":
                    cols = slice(g * HALF, (g + 1) * HALF)
                    return b0[:, cols], HALF, b0h[:, cols], b0l[:, cols]
                cols = slice(G0_START[g], G0_START[g] + G0_WIDTH[g])
                return m0[k * P:(k + 1) * P, cols], G0_WIDTH[g], w0h[:, k, cols], w0l[:, k, cols]

            pool_units = [("A", u, 0) for u in range(LORAS // 4)]
            pool_units += [("B", r, h) for r in range(LORAS * RANK // P) for h in range(2)]
            tables = len(pool_units)
            pool_units += [("W", k, g) for k in range(KC) for g in range(3)]

            def pool_places(n):
                kind, u, v = pool_units[n]
                if kind == "A":
                    src = a1[4 * u:4 * u + 4].rearrange("i p c -> p i c")
                    to = [a1_dram[4 * u:4 * u + 4, :, s * P:(s + 1) * P].rearrange("i p c -> p i c") for s in range(2)]
                elif kind == "B":
                    src = b1[u * P:(u + 1) * P, v * HALF:(v + 1) * HALF]
                    to = [b1_dram[u * P:(u + 1) * P, s, v * HALF:(v + 1) * HALF] for s in range(2)]
                else:
                    cols = slice(G1_AT[v], G1_AT[v] + G1_BASE[v])
                    src = w1t[u * P:(u + 1) * P, G1_COL[v]:G1_COL[v] + G1_BASE[v]]
                    return src, G1_BASE[v], w1h_k[:, u, cols], w1l_k[:, u, cols], None
                cols = slice(n * HALF, (n + 1) * HALF)
                return src, HALF, w1h[:, cols], w1l[:, cols], to

            def wq_cols(u):
                return slice((u % 2) * HALF, (u % 2 + 1) * HALF)

            with nc.Block() as block:

                @block.sync
                def _(sp):
                    sp.dma_start(ids0_sb[:, :], ids0.rearrange("(a n) -> a n", a=1)).then_inc(s_ids, 16)
                    sp.dma_start(xbuf[:, 0, :], x_t[0]).then_inc(x_loaded[0], 16)
                    sp.wait_ge(s_ids, 16)
                    sp.wait_ge(wbd_zeroed, 1)

                    def load_cond(t, b):
                        for j in range(PER_TILE):
                            which = sp.value_load(ids0_sb[0:1, bass.ds(PER_TILE * t + j, 1)], min_val=0, max_val=15)
                            rows = slice(j * CH, (j + 1) * CH)
                            sp.dma_start(wbd[rows, b, rows],
                                         wc[bass.ds(which, 1)].rearrange("a c d -> (a c) d")).then_inc(wc_loaded[b], 16)

                    load_cond(0, 0)
                    for n, unit in enumerate(w0_units):
                        src, width, _, _ = w0_places(unit)
                        if n >= 4:
                            sp.wait_ge(w0_lo, n - 3)
                        sp.dma_start(stage[n % 4][:, 0:width], src).then_inc(stage_loaded[n % 4], 16)
                        if n == 3:
                            sp.dma_start(b_base_sb[:, :], b_base.partition_broadcast(P)).then_inc(bias_loaded, 16)
                            sp.dma_start(s_in_sb[:, :], s_in.partition_broadcast(P)).then_inc(s_const, 16)
                            sp.dma_start(s_w_sb[:, :], s_w.partition_broadcast(P)).then_inc(s_const, 16)
                            sp.dma_start(xbuf[:, 1, :], x_t[1]).then_inc(x_loaded[1], 16)
                            load_cond(1, 1)
                    sp.dma_start(ids1_sb[:, :], ids1.rearrange("(a n) -> a n", a=1)).then_inc(s_ids, 16)

                    def tile(t, b, more):
                        sp.wait_ge(x1_done[2], t + 1)
                        sp.dma_start(x1_dram[bass.ds(t, 1)].rearrange("a p n -> (a p) n"),
                                     x1buf[:, b, :]).then_inc(x1_stored[b], 16)
                        if more:
                            sp.dma_start(xbuf[:, b, :], x_t[bass.ds(t + 2, 1)].rearrange("a p n -> (a p) n"))\
                              .then_inc(x_loaded[b], 16)
                            load_cond(t + 2, b)

                    tile(0, 0, True)
                    tile(1, 1, True)
                    with sp.Fori(2, TILES - 3, 2) as i:
                        tile(i, 0, True)
                        tile(i + 1, 1, True)
                    tile(TILES - 2, 0, False)
                    tile(TILES - 1, 1, False)
                    for b in range(2):
                        sp.wait_ge(x1_stored[b], 16 * TILES // 2)
                    sp.wait_ge(s_ids, 32)

                @block.gpsimd
                def _(pool):
                    pool.memset(wbd[:, :, :], 0.0).then_inc(wbd_zeroed, 1)
                    pool.memset(ident[:, :], 0.0).then_inc(s_ident, 1)
                    pool.memset(ident_b[:, :], 0.0).then_inc(s_ident, 1)
                    pool.wait_ge(s_ident, 2)
                    for m in (ident, ident_b):
                        pool.affine_select(out=m[:, :], in_=m[:, :], compare_op=ALU.not_equal, fill=1.0, base=0,
                                           pattern=[[-1, P]], channel_multiplier=1).then_inc(s_ident, 1)
                    for n in range(2):
                        src, width, _, _, _ = pool_places(n)
                        pool.dma_start(pool_raw[:, n % 2, 0:width], src).then_inc(pool_loaded[n % 2], 16)
                    for u in range(2):
                        pool.dma_start(wq_val[:, u, :], wf[0:P, wq_cols(u)]).then_inc(wq_loaded[u], 16)
                    pool.wait_ge(bias_loaded, 16)

                    def add_bias(t, b):
                        pool.wait_ge(y_ps[1], t + 1)
                        pool.tensor_tensor(xbuf[:, b, :], xbuf[:, b, :], b_base_sb[:, :], ALU.add).then_inc(xb_done, 1)

                    def split(n):
                        src, width, hi, lo, to = pool_places(n)
                        raw = pool_raw[:, n % 2, 0:width]
                        pool.wait_ge(pool_loaded[n % 2], 16 * (n // 2 + 1))
                        if n == tables:
                            pool.wait_ge(split_stored, 32 * tables)
                        pool.tensor_scalar(hi, raw, 1.0, None, ALU.mult).then_inc(pool_hi, 1)
                        pool.wait_ge(pool_hi, n + 1)
                        pool.tensor_tensor(lo, raw, hi, ALU.subtract).then_inc(pool_lo, 1)
                        pool.wait_ge(pool_lo, n + 1)
                        if to:
                            for dram, part in zip(to, (hi.bitcast(F32), lo.bitcast(F32))):
                                if pool_units[n][0] == "A":
                                    part = part.rearrange("p (i c) -> p i c", i=4)
                                pool.dma_start(dram, part).then_inc(split_stored, 16)
                        if n + 2 < len(pool_units):
                            src, width, _, _, _ = pool_places(n + 2)
                            pool.dma_start(pool_raw[:, n % 2, 0:width], src).then_inc(pool_loaded[n % 2], 16)

                    units = list(range(len(pool_units)))
                    t = 0
                    while units or t <= WQ_TILES[-1] or t % 2:
                        add_bias(t, t % 2)
                        if t - 1 in WQ_TILES:
                            done = 2 * (WQ_TILES.index(t - 1) + 1)
                            pool.wait_ge(wq_step, 7 * done)
                            for u in range(done, min(done + 2, 2 * KC)):
                                pool.dma_start(wq_val[:, u % 2, :], wf[u // 2 * P:(u // 2 + 1) * P, wq_cols(u)])\
                                    .then_inc(wq_loaded[u % 2], 16)
                        for _ in range(min(POOL_UNITS_A_TILE, len(units))):
                            split(units.pop(0))
                        t += 1
                    with pool.Fori(t, TILES - 1, 2) as i:
                        add_bias(i, 0)
                        add_bias(i + 1, 1)

                @block.scalar
                def _(act):
                    def y_hi(t):
                        for h in range(2):
                            act.wait_ge(y_ps[h], t + 1)
                            act.activation(yh[:, h * HALF:(h + 1) * HALF], bank_t[:, h, :], ACT.Copy)\
                               .then_inc(yh_done[h], 1)

                    for n, unit in enumerate(w0_units):
                        _, width, hi, _ = w0_places(unit)
                        act.wait_ge(stage_loaded[n % 4], 16 * (n // 4 + 1))
                        act.activation(hi, stage[n % 4][:, 0:width], ACT.Copy,
                                       scale=LORA_SCALE if unit[0] == "b" else 1.0).then_inc(w0_hi, 1)
                        if n == 1:
                            y_hi(0)

                    def tile(t, more):
                        act.wait_ge(negmax_done, t + 1)
                        act.activation(expo[:, :], bank_g[:, 0, ER:ER + EXPERTS], ACT.Exp, bias=negmax[:, :],
                                       accum_out=esum[:, :]).then_inc(exp_done, 1)
                        act.wait_ge(hwt_ps, t + 1)
                        act.activation(hwt_h[:, :], bank_m[:, 0:P], ACT.Copy).then_inc(hwth_done, 1)
                        if more:
                            y_hi(t + 1)

                    tile(0, True)
                    tile(1, True)
                    with act.Fori(2, TILES - 3, 2) as i:
                        tile(i, True)
                        tile(i + 1, True)
                    tile(TILES - 2, True)
                    tile(TILES - 1, False)

                @block.vector
                def _(dve):
                    dve.memset(probs[:, :], -1.0).then_inc(probs_done, 1)
                    dve.memset(to_replace[:, :], -1.0).then_inc(replace_done, 1)
                    dve.memset(slot_mask[:, :], 0.0).then_inc(mask_set, 1)
                    dve.wait_ge(mask_set, 1)
                    for j in range(PER_TILE):
                        dve.memset(slot_mask[j * CH:(j + 1) * CH, j * RANK:(j + 1) * RANK], 1.0).then_inc(mask_set, 1)

                    def y_lo(t):
                        for h in range(2):
                            half = slice(h * HALF, (h + 1) * HALF)
                            dve.wait_ge(yh_done[h], t + 1)
                            dve.tensor_tensor(yl[:, half], bank_t[:, h, :], yh[:, half], ALU.subtract)\
                               .then_inc(yl_done[h], 1)

                    for n, unit in enumerate(w0_units):
                        _, width, hi, lo = w0_places(unit)
                        dve.wait_ge(w0_hi, n + 1)
                        raw = stage[n % 4][:, 0:width]
                        if unit[0] == "b":
                            dve.scalar_tensor_tensor(lo, raw, LORA_SCALE, hi, ALU.mult, ALU.subtract).then_inc(w0_lo, 1)
                        else:
                            dve.tensor_tensor(lo, raw, hi, ALU.subtract).then_inc(w0_lo, 1)
                        if n == 1:
                            y_lo(0)
                    dve.wait_ge(s_const, 32)
                    dve.reciprocal(inv_in[:, :], s_in_sb[:, :]).then_inc(s_scale, 1)
                    dve.reciprocal(inv_w[:, :], s_w_sb[:, :]).then_inc(s_scale, 1)
                    dve.tensor_tensor(s_out[:, :], s_in_sb[:, :], s_w_sb[:, :], ALU.mult).then_inc(s_scale, 1)
                    dve.wait_ge(s_scale, 3)

                    def quantize_weight(u):
                        val = wq_val[:, u % 2, :]
                        power = wq_pow[:, :]
                        to = wq[:, u // 2, wq_cols(u)]
                        base = 7 * u
                        dve.wait_ge(wq_loaded[u % 2], 16 * (u // 2 + 1))
                        dve.tensor_scalar(val, val, inv_w[:, :], None, ALU.mult).then_inc(wq_step, 1)
                        dve.wait_ge(wq_step, base + 1)
                        dve.tensor_scalar(power.bitcast(U32), val.bitcast(U32), 0x7F800000, None, ALU.bitwise_and)\
                           .then_inc(wq_step, 1)
                        dve.wait_ge(wq_step, base + 2)
                        dve.tensor_scalar(power, power, MIN_NORMAL, ROUND_C, ALU.max, ALU.mult).then_inc(wq_step, 1)
                        dve.wait_ge(wq_step, base + 3)
                        dve.tensor_tensor(val, val, power, ALU.add).then_inc(wq_step, 1)
                        dve.wait_ge(wq_step, base + 4)
                        dve.tensor_tensor(to, val, power, ALU.subtract).then_inc(wq_step, 1)
                        dve.wait_ge(wq_step, base + 5)
                        dve.tensor_scalar(wq_nan, to, OVERFLOW_C, 0.0, ALU.mult, ALU.mult).then_inc(wq_step, 1)
                        dve.wait_ge(wq_step, base + 6)
                        dve.tensor_tensor(to, to, wq_nan, ALU.add).then_inc(wq_step, 1)

                    def tile(t, b, stored, more, wq_units=()):
                        n = t + 1
                        dve.wait_ge(h_ps, n)
                        dve.tensor_reduce(negmax[:, :], bank_g[:, 0, ER:ER + EXPERTS], AXIS.X, ALU.max, negate=True)\
                           .then_inc(negmax_done, 1)
                        dve.wait_ge(exp_done, n)
                        dve.reciprocal(rsum[:, :], esum[:, :]).then_inc(rsum_done, 1)
                        dve.max(sorted8[:, :], expo[:, :]).then_inc(sorted_done, 1)
                        dve.wait_ge(rsum_done, n)
                        dve.tensor_scalar(probs[:, 0:EXPERTS], expo[:, :], rsum[:, :], None, ALU.mult)\
                           .then_inc(probs_done, 1)
                        dve.wait_ge(sorted_done, n)
                        dve.tensor_scalar(to_replace[:, 0:2], sorted8[:, 0:2], rsum[:, :], None, ALU.mult)\
                           .then_inc(replace_done, 1)
                        dve.wait_ge(probs_done, n + 1)
                        dve.wait_ge(replace_done, n + 1)
                        dve.tensor_tensor(top_sum[:, :], to_replace[:, 0:1], to_replace[:, 1:2], ALU.add)\
                           .then_inc(top_sum_done, 1)
                        dve.match_replace(without_top[:, :], to_replace[:, :], probs[:, :], 0.0)\
                           .then_inc(without_done, 1)
                        dve.wait_ge(top_sum_done, n)
                        dve.reciprocal(top_inv[:, :], top_sum[:, :]).then_inc(top_inv_done, 1)
                        dve.wait_ge(without_done, n)
                        dve.tensor_tensor(top_probs[:, :], probs[:, 0:EXPERTS], without_top[:, 0:EXPERTS],
                                          ALU.subtract).then_inc(top_done, 1)
                        dve.wait_ge(top_done, n)
                        dve.wait_ge(top_inv_done, n)
                        gate = top_probs[:, :].unsqueeze(2).to_broadcast([P, EXPERTS, RANK])
                        dve.scalar_tensor_tensor(hw[:, :].rearrange("p (e r) -> p e r", r=RANK),
                                                 bank_g[:, 0, 0:ER].rearrange("p (e r) -> p e r", r=RANK),
                                                 top_inv[:, :], gate, ALU.mult, ALU.mult).then_inc(hw_done, 1)
                        for u in wq_units[0:1]:
                            quantize_weight(u)
                        dve.wait_ge(hwth_done, n)
                        dve.tensor_tensor(hwt_l[:, :], bank_m[:, 0:P], hwt_h[:, :], ALU.subtract).then_inc(hwtl_done, 1)
                        for u in wq_units[1:2]:
                            quantize_weight(u)
                        if more:
                            y_lo(n)
                        dve.wait_ge(xb_done, n)
                        if stored is not None:
                            dve.wait_ge(x1_stored[b], stored)
                        for g in range(3):
                            dve.wait_ge(acc_ps[g], n)
                            width = G0_WIDTH[g] - G0_OUT[g]
                            cols = slice(G0_COL[g], G0_COL[g] + width)
                            dve.tensor_tensor(x1buf[:, b, cols], bank_g[:, g, G0_OUT[g]:G0_WIDTH[g]],
                                              xbuf[:, b, cols], ALU.add).then_inc(x1_done[g], 1)

                    units = list(range(2 * KC))
                    first = WQ_TILES[-1] + 1
                    for t in range(first):
                        tile(t, t % 2, 16 * (t // 2) if t >= 2 else None, True,
                             [units.pop(0), units.pop(0)] if t in WQ_TILES else ())
                    with dve.Fori(first, TILES - 3, 2) as i:
                        tile(i, 0, 8 * i, True)
                        tile(i + 1, 1, 8 * i, True)
                    tile(TILES - 2, 0, 8 * (TILES - 2), True)
                    tile(TILES - 1, 1, 8 * (TILES - 2), False)

                @block.tensor
                def _(pe):
                    def cond(t, b, loads):
                        pe.wait_ge(x_loaded[b], 16 * loads)
                        pe.wait_ge(wc_loaded[b], 32 * loads)
                        for k in range(KC):
                            cols = slice((k % 4) * P, (k % 4 + 1) * P)
                            last = pe.matmul(bank_t[:, k // 4, cols], xbuf[:, b, k * P:(k + 1) * P], wbd[:, b, :],
                                             start=True, stop=True)
                            if k % 4 == 3:
                                last.then_inc(y_ps[k // 4], 1)

                    def bank(g):
                        cols = slice(G0_START[g], G0_START[g] + G0_WIDTH[g])
                        to = bank_g[:, g, 0:G0_WIDTH[g]]
                        for k in range(KC):
                            rows = slice(k * P, (k + 1) * P)
                            pe.matmul(to, yh[:, rows], w0h[:, k, cols], start=(k == 0), stop=False)
                            pe.matmul(to, yh[:, rows], w0l[:, k, cols], start=False, stop=False)
                            last = pe.matmul(to, yl[:, rows], w0h[:, k, cols], start=False, stop=(k == KC - 1))
                        return last

                    def tile(t, b, loads, prior, more):
                        n = t + 1
                        for h in range(2):
                            pe.wait_ge(yl_done[h], n)
                        for g in range(3):
                            if prior:
                                pe.wait_ge(x1_done[g], t)
                            else:
                                pe.wait_ge(w0_lo, w0_need[g])
                            last = bank(g)
                            if g == 0:
                                last.then_inc(h_ps, 1)
                            if g == 1:
                                pe.wait_ge(hw_done, n)
                                pe.transpose(bank_m[:, 0:P], hw[:, :], ident[:, :]).then_inc(hwt_ps, 1)
                        if more:
                            cond(n, 1 - b, loads)
                        pe.wait_ge(hwtl_done, n)
                        for g in range(3):
                            to = bank_g[:, g, G0_OUT[g]:G0_WIDTH[g]]
                            cols = slice(G0_COL[g], G0_COL[g] + G0_WIDTH[g] - G0_OUT[g])
                            pe.matmul(to, hwt_h[:, :], b0h[:, cols], start=False, stop=False, skip_group_check=True)
                            pe.matmul(to, hwt_h[:, :], b0l[:, cols], start=False, stop=False, skip_group_check=True)
                            pe.matmul(to, hwt_l[:, :], b0h[:, cols], start=False, stop=True, skip_group_check=True)\
                              .then_inc(acc_ps[g], 1)

                    pe.wait_ge(s_ident, 4)
                    cond(0, 0, 1)
                    tile(0, 0, 1, False, True)
                    tile(1, 1, 2, True, True)
                    with pe.Fori(2, TILES - 3, 2) as i:
                        half = pe.snap(i // 2)
                        tile(i, 0, half + 1, True, True)
                        tile(i + 1, 1, half + 2, True, True)
                    tile(TILES - 2, 0, TILES // 2, True, True)
                    tile(TILES - 1, 1, None, True, False)

        with ExitStack() as p2:
            xin = sb("xin", [P, 2, D], F32, p2)
            obuf = sb("obuf", [P, 2, D], F32, p2)
            xh = sb("xh", [P, D], F32R, p2)
            xl = sb("xl", [P, D], F32R, p2)
            a_raw = sb("a_raw", [P, 2, PER_TILE, 2 * KC * RANK], F32, p2)
            b_stack = [sb(f"b_stack{b}", [STACK, D], F32R, p2) for b in range(2)]
            ones = sb("ones", [P, 1], F32, p2)
            h_masked = sb("h_masked", [P, LR], F32, p2)
            h_stack = sb("h_stack", [P, STACK], F32, p2)
            ht = sb("ht", [STACK, P], F32R, p2)
            val = sb("val", [P, D], F32, p2)
            power = sb("power", [P, D], F32, p2)
            rounded = sb("rounded", [P, D], BF16, p2)
            nan_or_0 = sb("nan_or_0", [P, D], BF16, p2)
            rq = sb("rq", [P, D], BF16, p2)
            rqt = sb("rqt", [P, D], BF16, p2)
            bias2_sb = sb("bias2_sb", [P, D], F32, p2)
            bias_raw = sb("bias_raw", [1, D], F32, p2)
            bias_h = sb("bias_h", [1, D], F32R, p2)
            bias_l = sb("bias_l", [1, D], F32R, p2)

            x1_loaded = [sem(f"x1_loaded{b}") for b in range(2)]
            a_loaded = [sem(f"a_loaded{b}") for b in range(2)]
            b_loaded = [sem(f"b_loaded{b}") for b in range(2)]
            slot_done = sem("slot_done")
            bias2_loaded = sem("bias2_loaded")
            bias_loaded2 = sem("bias_loaded2")
            bias_split = sem("bias_split")
            bias_rows = sem("bias_rows")
            xt_ps = [sem(f"xt_ps{h}") for h in range(2)]
            xh_done = [sem(f"xh_done{h}") for h in range(2)]
            xl_done = [sem(f"xl_done{h}") for h in range(2)]
            h1_ps = sem("h1_ps")
            masked_done = sem("masked_done")
            h_hi_done = sem("h_hi_done")
            h_ones = sem("h_ones")
            stack_done = sem("stack_done")
            ht_ps = sem("ht_ps")
            ht_done = sem("ht_done")
            r_ps = [sem(f"r_ps{g}") for g in range(3)]
            val_done = [sem(f"val_done{g}") for g in range(3)]
            power_done = sem("power_done")
            scaled_done = sem("scaled_done")
            shifted_done = sem("shifted_done")
            rounded_done = sem("rounded_done")
            nan_done = sem("nan_done")
            rq_done = sem("rq_done")
            rqt_ps = sem("rqt_ps")
            rqt_done = sem("rqt_done")
            f_ps = [sem(f"f_ps{h}") for h in range(2)]
            x1b_done = sem("x1b_done")
            out_done = [sem(f"out_done{h}") for h in range(2)]
            out_stored = [sem(f"out_stored{b}") for b in range(2)]

            with nc.Block() as block:

                @block.sync
                def _(sp):
                    def load_x1(t, b):
                        sp.dma_start(xin[:, b, :], x1_dram[bass.ds(t, 1)].rearrange("a p n -> (a p) n"))\
                          .then_inc(x1_loaded[b], 16)

                    def load_adapters(t, b):
                        for j in range(PER_TILE):
                            which = sp.value_load(ids1_sb[0:1, bass.ds(PER_TILE * t + j, 1)],
                                                  min_val=0, max_val=LORAS - 1)
                            sp.dma_start(a_raw[:, b, j, :], a1_dram[bass.ds(which, 1)].rearrange("a p c -> (a p) c"))\
                              .then_inc(a_loaded[b], 16)
                            for s, part in enumerate((0, 0, 1)):
                                row = s * LR + j * RANK
                                sp.dma_start(b_stack[b][row:row + RANK, :].bitcast(F32),
                                             b1_ids[bass.ds(which, 1), :, part, :].rearrange("a r n -> (a r) n"))\
                                  .then_inc(b_loaded[b], 16)

                    load_x1(0, 0)
                    load_adapters(0, 0)
                    sp.dma_start(bias_raw[:, :], base_bias.rearrange("(a n) -> a n", a=1)).then_inc(bias_loaded2, 16)
                    sp.dma_start(bias2_sb[:, :], bias2.partition_broadcast(P)).then_inc(bias2_loaded, 16)
                    load_x1(1, 1)
                    sp.wait_ge(bias_split, 2)
                    for b in range(2):
                        for s, part in enumerate((bias_h, bias_l)):
                            sp.dma_start(b_stack[b][3 * LR + s:3 * LR + s + 1, :].bitcast(F32),
                                         part[:, :].bitcast(F32)).then_inc(bias_rows, 16)

                    def store_out(t, b):
                        sp.wait_ge(out_done[1], t + 1)
                        sp.dma_start(out_t[bass.ds(t, 1)].rearrange("a p n -> (a p) n"), obuf[:, b, :])\
                          .then_inc(out_stored[b], 16)

                    def tile(t, b, lag, more):
                        if lag:
                            sp.wait_ge(r_ps[2], t)
                            sp.wait_ge(slot_done, t)
                        if more != 0:
                            load_adapters(t + 1, 1 - b)
                        if lag == 2:
                            store_out(t - 2, b)
                        if more == 2:
                            sp.wait_ge(xt_ps[1], t + 1)
                            sp.wait_ge(x1b_done, t + 1)
                            load_x1(t + 2, b)

                    tile(0, 0, 0, 2)
                    tile(1, 1, 1, 2)
                    with sp.Fori(2, TILES - 3, 2) as i:
                        tile(i, 0, 2, 2)
                        tile(i + 1, 1, 2, 2)
                    tile(TILES - 2, 0, 2, 1)
                    tile(TILES - 1, 1, 2, 0)
                    store_out(TILES - 2, 0)
                    store_out(TILES - 1, 1)
                    for b in range(2):
                        sp.wait_ge(out_stored[b], 16 * TILES // 2)

                @block.gpsimd
                def _(pool):
                    pool.memset(h_stack[:, :], 1.0).then_inc(h_ones, 1)
                    pool.memset(ones[:, :], 1.0).then_inc(h_ones, 1)
                    pool.wait_ge(h_ones, 2)
                    one = ones[:, :].unsqueeze(2)

                    def fill_slot(t, b, loads, lag):
                        pool.wait_ge(a_loaded[b], 32 * loads)
                        if lag:
                            pool.wait_ge(h1_ps, t - 1)
                        at = b * (LR + G1_BASE[0])
                        for s, w in enumerate((w1h_k, w1l_k)):
                            to = w[:, :, at:at + LR].rearrange("p k (j r) -> p j k r", j=PER_TILE)
                            for j in range(PER_TILE):
                                part = a_raw[:, b, j, s * P:(s + 1) * P].rearrange("p (k r) -> p k r", r=RANK)
                                last = pool.tensor_tensor(to[:, j], part, one.to_broadcast([P, KC, RANK]), ALU.mult)
                        last.then_inc(slot_done, 1)

                    fill_slot(0, 0, 1, False)
                    pool.wait_ge(bias2_loaded, 16)

                    def tile(t, b, loads, stored, lag, more):
                        pool.wait_ge(x1_loaded[b], 16 * loads)
                        if stored is not None:
                            pool.wait_ge(out_stored[b], stored)
                        pool.tensor_tensor(obuf[:, b, :], xin[:, b, :], bias2_sb[:, :], ALU.add).then_inc(x1b_done, 1)
                        if more:
                            fill_slot(t + 1, 1 - b, loads if b == 0 else loads + 1, lag)

                    tile(0, 0, 1, None, False, True)
                    tile(1, 1, 1, None, True, True)
                    with pool.Fori(2, TILES - 3, 2) as i:
                        half = pool.snap(i // 2)
                        tile(i, 0, half + 1, 8 * i, True, True)
                        tile(i + 1, 1, half + 1, 8 * i, True, True)
                    tile(TILES - 2, 0, TILES // 2, 8 * (TILES - 2), True, True)
                    tile(TILES - 1, 1, TILES // 2, 8 * (TILES - 2), True, False)

                @block.scalar
                def _(act):
                    act.wait_ge(bias_loaded2, 16)
                    act.activation(bias_h[:, :], bias_raw[:, :], ACT.Copy).then_inc(bias_split, 1)

                    def x_hi(t):
                        for h in range(2):
                            act.wait_ge(xt_ps[h], t + 1)
                            act.activation(xh[:, h * HALF:(h + 1) * HALF], bank_t[:, h, :], ACT.Copy)\
                               .then_inc(xh_done[h], 1)

                    def rq_out(t):
                        act.wait_ge(rqt_ps, t + 1)
                        act.activation(rqt[:, :], rq_ps, ACT.Copy).then_inc(rqt_done, 1)

                    def tile(t, b, lag, more):
                        act.wait_ge(ht_ps, t + 1)
                        act.activation(ht[:, :], bank_f[0:STACK, 0, 0:P], ACT.Copy).then_inc(ht_done, 1)
                        if lag:
                            rq_out(t - 1)
                        if more:
                            x_hi(t + 1)
                        if lag:
                            act.wait_ge(rounded_done, t)
                        for g in range(3):
                            act.wait_ge(r_ps[g], t + 1)
                            at = LR if g == 0 and b == 0 else 0
                            act.activation(val[:, G1_COL[g]:G1_COL[g] + G1_BASE[g]],
                                           bank_g[:, g, at:at + G1_BASE[g]], ACT.Copy, scale=inv_in[:, :])\
                               .then_inc(val_done[g], 1)

                    x_hi(0)
                    tile(0, 0, False, True)
                    tile(1, 1, True, True)
                    with act.Fori(2, TILES - 3, 2) as i:
                        tile(i, 0, True, True)
                        tile(i + 1, 1, True, True)
                    tile(TILES - 2, 0, True, True)
                    tile(TILES - 1, 1, True, False)
                    rq_out(TILES - 1)

                @block.vector
                def _(dve):
                    def x_lo(t):
                        for h in range(2):
                            half = slice(h * HALF, (h + 1) * HALF)
                            dve.wait_ge(xh_done[h], t + 1)
                            dve.tensor_tensor(xl[:, half], bank_t[:, h, :], xh[:, half], ALU.subtract)\
                               .then_inc(xl_done[h], 1)

                    def quantize(t):
                        n = t + 1
                        dve.wait_ge(val_done[2], n)
                        dve.tensor_scalar(power[:, :].bitcast(U32), val[:, :].bitcast(U32), 0x7F800000, None,
                                          ALU.bitwise_and).then_inc(power_done, 1)
                        dve.wait_ge(power_done, n)
                        dve.tensor_scalar(power[:, :], power[:, :], MIN_NORMAL, ROUND_C, ALU.max, ALU.mult)\
                           .then_inc(scaled_done, 1)
                        dve.wait_ge(scaled_done, n)
                        dve.tensor_tensor(val[:, :], val[:, :], power[:, :], ALU.add).then_inc(shifted_done, 1)
                        dve.wait_ge(shifted_done, n)
                        dve.tensor_tensor(rounded[:, :], val[:, :], power[:, :], ALU.subtract)\
                           .then_inc(rounded_done, 1)
                        dve.wait_ge(rounded_done, n)
                        dve.tensor_scalar(nan_or_0[:, :], rounded[:, :], OVERFLOW_C, 0.0, ALU.mult, ALU.mult)\
                           .then_inc(nan_done, 1)
                        dve.wait_ge(nan_done, n)
                        dve.tensor_tensor(rq[:, :], rounded[:, :], nan_or_0[:, :], ALU.add).then_inc(rq_done, 1)

                    def finish(t, b):
                        dve.wait_ge(x1b_done, t + 1)
                        for h in range(2):
                            half = slice(h * HALF, (h + 1) * HALF)
                            dve.wait_ge(f_ps[h], t + 1)
                            dve.scalar_tensor_tensor(obuf[:, b, half], bank_f[:, h, :], s_out[:, :],
                                                     obuf[:, b, half], ALU.mult, ALU.add).then_inc(out_done[h], 1)

                    def stack_h(t, b):
                        n = t + 1
                        at = 0 if b == 0 else G1_BASE[0]
                        dve.wait_ge(h1_ps, n)
                        dve.tensor_tensor(h_masked[:, :], bank_g[:, 0, at:at + LR], slot_mask[:, :], ALU.mult)\
                           .then_inc(masked_done, 1)
                        dve.wait_ge(masked_done, n)
                        for s in (0, 2):
                            last = dve.tensor_copy(h_stack[:, s * LR:(s + 1) * LR].bitcast(F32R), h_masked[:, :])
                        last.then_inc(h_hi_done, 1)
                        dve.wait_ge(h_hi_done, n)
                        dve.tensor_tensor(h_stack[:, LR:2 * LR], h_masked[:, :], h_stack[:, 0:LR], ALU.subtract)\
                           .then_inc(stack_done, 1)

                    def tile(t, b, lag, more):
                        if lag >= 1:
                            quantize(t - 1)
                        if lag >= 2:
                            finish(t - 2, b)
                        stack_h(t, b)
                        if more:
                            x_lo(t + 1)

                    dve.wait_ge(bias_split, 1)
                    dve.tensor_tensor(bias_l[:, :], bias_raw[:, :], bias_h[:, :], ALU.subtract).then_inc(bias_split, 1)
                    x_lo(0)
                    dve.wait_ge(h_ones, 2)
                    tile(0, 0, 0, True)
                    tile(1, 1, 1, True)
                    with dve.Fori(2, TILES - 3, 2) as i:
                        tile(i, 0, 2, True)
                        tile(i + 1, 1, 2, True)
                    tile(TILES - 2, 0, 2, True)
                    tile(TILES - 1, 1, 2, False)
                    quantize(TILES - 1)
                    finish(TILES - 2, 0)
                    finish(TILES - 1, 1)

                @block.tensor
                def _(pe):
                    def transpose_x(t, b, loads):
                        pe.wait_ge(x1_loaded[b], 16 * loads)
                        for k in range(KC):
                            cols = slice((k % 4) * P, (k % 4 + 1) * P)
                            last = pe.transpose(bank_t[:, k // 4, cols], xin[:, b, k * P:(k + 1) * P], ident[:, :])
                            if k % 4 == 3:
                                last.then_inc(xt_ps[k // 4], 1)

                    def bank(g, b):
                        if g == 0:
                            cols = slice(b * LR, b * LR + LR + G1_BASE[0])
                        else:
                            cols = slice(G1_AT[g], G1_AT[g] + G1_BASE[g])
                        to = bank_g[:, g, 0:cols.stop - cols.start]
                        for k in range(KC):
                            rows = slice(k * P, (k + 1) * P)
                            pe.matmul(to, xh[:, rows], w1h_k[:, k, cols], start=(k == 0), stop=False)
                            pe.matmul(to, xh[:, rows], w1l_k[:, k, cols], start=False, stop=False)
                            last = pe.matmul(to, xl[:, rows], w1h_k[:, k, cols], start=False, stop=(k == KC - 1))
                        return last

                    def transpose_rq(t):
                        pe.wait_ge(rq_done, t + 1)
                        for k in range(KC):
                            rows = slice(k * P, (k + 1) * P)
                            last = pe.transpose(rq_ps[:, rows], rq[:, rows], ident_b[:, :])
                        last.then_inc(rqt_ps, 1)

                    def ffn(t):
                        pe.wait_ge(rqt_done, t + 1)
                        for h in range(2):
                            for k in range(KC):
                                last = pe.matmul(bank_f[:, h, :], rqt[:, k * P:(k + 1) * P],
                                                 wq[:, k, h * HALF:(h + 1) * HALF], start=(k == 0), stop=(k == KC - 1))
                            last.then_inc(f_ps[h], 1)

                    def tile(t, b, loads, lag, more):
                        n = t + 1
                        for h in range(2):
                            pe.wait_ge(xl_done[h], n)
                        pe.wait_ge(slot_done, n)
                        for g in range(3):
                            if lag:
                                pe.wait_ge(val_done[g], t)
                            last = bank(g, b)
                            if g == 0:
                                last.then_inc(h1_ps, 1)
                            if g == 1:
                                if lag == 2:
                                    pe.wait_ge(out_done[1], t - 1)
                                pe.wait_ge(stack_done, n)
                                pe.transpose(bank_f[0:STACK, 0, 0:P], h_stack[:, :], ident[:, :]).then_inc(ht_ps, 1)
                                if lag:
                                    transpose_rq(t - 1)
                        if more:
                            transpose_x(n, 1 - b, loads if b == 0 else loads + 1)
                        pe.wait_ge(b_loaded[b], 96 * loads)
                        pe.wait_ge(ht_done, n)
                        for g in range(3):
                            at = LR if g == 0 and b == 0 else 0
                            pe.matmul(bank_g[:, g, at:at + G1_BASE[g]], ht[:, :],
                                      b_stack[b][:, G1_COL[g]:G1_COL[g] + G1_BASE[g]],
                                      start=False, stop=True, skip_group_check=True).then_inc(r_ps[g], 1)
                        if lag:
                            ffn(t - 1)

                    transpose_x(0, 0, 1)
                    pe.wait_ge(bias_rows, 64)
                    tile(0, 0, 1, 0, True)
                    tile(1, 1, 1, 1, True)
                    with pe.Fori(2, TILES - 3, 2) as i:
                        half = pe.snap(i // 2)
                        tile(i, 0, half + 1, 2, True)
                        tile(i + 1, 1, half + 1, 2, True)
                    tile(TILES - 2, 0, TILES // 2, 2, True)
                    tile(TILES - 1, 1, TILES // 2, 2, False)
                    transpose_rq(TILES - 1)
                    pe.wait_ge(out_done[1], TILES - 1)
                    ffn(TILES - 1)


def kernel(x, itok_B_0_15, itok_B_6_15, L0_cond_weights, L0_ffn_W_base, L0_ffn_b_base, L0_ffn_W_router,
           L0_ffn_A, L0_ffn_B, L1_cond_base_weight, L1_cond_base_bias, L1_cond_lora_A_w, L1_cond_lora_B_w,
           L1_ffn_weight, L1_ffn_bias, L1_ffn_input_scale, L1_ffn_weight_scale):
    import concourse.bacc as bacc
    from concourse.bass_utils import run_bass_kernel_spmd

    def lay(a):
        return np.ascontiguousarray(a)

    a_w = np.asarray(L1_cond_lora_A_w)
    arrays = {
        "x": lay(x),
        "ids0": lay(itok_B_0_15),
        "ids1": lay(itok_B_6_15),
        "wc": lay(L0_cond_weights),
        "m0": lay(np.concatenate([np.asarray(L0_ffn_A).reshape(ER, D), np.asarray(L0_ffn_W_router),
                                  np.asarray(L0_ffn_W_base)]).T),
        "b0": lay(np.asarray(L0_ffn_B).transpose(0, 2, 1).reshape(ER, D)),
        "b_base": lay(L0_ffn_b_base),
        "w1t": lay(np.asarray(L1_cond_base_weight).T),
        "base_bias": lay(L1_cond_base_bias),
        "a1": lay(a_w.reshape(LORAS, RANK, KC, P).transpose(0, 3, 2, 1).reshape(LORAS, P, KC * RANK)),
        "b1": lay(np.asarray(L1_cond_lora_B_w).transpose(0, 2, 1).reshape(LORAS * RANK, D)),
        "wf": lay(L1_ffn_weight),
        "bias2": lay(L1_ffn_bias),
        "s_in": lay(L1_ffn_input_scale),
        "s_w": lay(L1_ffn_weight_scale),
    }
    nc = bacc.Bacc("TRN2", target_bir_lowering=False, num_devices=1)
    args = {n: nc.dram_tensor(n, a.shape, mybir.dt.from_np(a.dtype), kind="ExternalInput").ap()
            for n, a in arrays.items()}
    out = nc.dram_tensor("out", (BATCH, CH, D), F32, kind="ExternalOutput").ap()
    build(nc, out=out, **args)
    r = run_bass_kernel_spmd(nc, [arrays], core_ids=[0])
    return r.results[0]["out"]
```

```python
from contextlib import ExitStack

import numpy as np

import concourse.bass as bass
from concourse import mybir

F32 = mybir.dt.float32
F32R = mybir.dt.float32r
BF16 = mybir.dt.bfloat16
U32 = mybir.dt.uint32
I32 = mybir.dt.int32
ALU = mybir.AluOpType
ACT = mybir.ActivationFunctionType
AXIS = mybir.AxisListType

P = 128
BATCH, CH, D = 128, 64, 1024
TILES = BATCH * CH // P
PER_TILE = P // CH
KC = D // P
HALF = 512
EXPERTS, RANK = 8, 16
ER = EXPERTS * RANK
LORA_SCALE = 2.0
LORAS = 32
LR = PER_TILE * RANK

G0_START = (0, 392, 776)
G0_WIDTH = (392, 384, 384)
G0_OUT = (ER + EXPERTS, 0, 0)
G0_COL = (0, 256, 640)
W0_COLS = ER + EXPERTS + D

G1_BASE = (320, 352, 352)
G1_COL = (0, 320, 672)
G1_AT = (LR, 2 * LR + 320, 2 * LR + 320 + 352)
W1_COLS = 2 * LR + D
STACK = 3 * LR + 2

ROUND_C = 1.5 * 2.0 ** 20
MIN_NORMAL = 2.0 ** -6
OVERFLOW_C = float(np.float32(2.0 ** 127 / 235.0))

PREP_TILES = 14
WQ_TILES = range(2, 10)
WQ_STEPS = 7
POOL_PIECES_A_TILE = 3


def row_of(t):
    return t - 2 if t >= 2 else TILES - 2 + t


def wq_pieces(t):
    return [2 * WQ_TILES.index(t) + u for u in range(2)] if t in WQ_TILES else []


def build(nc, x, ids0, ids1, wc, m0, b0, b_base, w1t, base_bias, a1, b1, wf, bias2, s_in, s_w, out):
    x_t = x.rearrange("b c t -> (b c) t").rearrange("(n p) t -> n p t", p=P)
    out_t = out.rearrange("b c t -> (b c) t").rearrange("(n p) t -> n p t", p=P)
    x1_dram = nc.dram_tensor("x1_scratch", (TILES, P, D), F32, kind="Internal").ap()
    a1_dram = nc.dram_tensor("a1_split", (LORAS, P, 2 * KC * RANK), F32, kind="Internal").ap()
    b1_dram = nc.dram_tensor("b1_split", (LORAS * RANK, 2, D), F32, kind="Internal").ap()
    b1_ids = b1_dram.rearrange("(i r) s n -> i r s n", r=RANK)

    with ExitStack() as whole:
        def sb(name, shape, dt, stack=whole):
            return stack.enter_context(nc.sbuf_tensor(name, shape, dt))

        def sem(name):
            return whole.enter_context(nc.semaphore(name))

        bank_g = whole.enter_context(nc.psum_tensor("bank_g", [P, 3, 512], F32))
        bank_t = whole.enter_context(nc.psum_tensor("bank_t", [P, 2, 512], F32))
        bank_f = whole.enter_context(nc.psum_tensor("bank_f", [P, 2, 512], F32))
        bank_m = whole.enter_context(nc.psum_tensor("bank_m", [P, 512], F32))
        rq_ps = bank_m[:, :].bitcast(BF16)

        w1h = sb("w1h", [P, KC * W1_COLS], F32R)
        w1l = sb("w1l", [P, KC * W1_COLS], F32R)
        w1h_k = w1h[:, :].rearrange("p (k n) -> p k n", k=KC)
        w1l_k = w1l[:, :].rearrange("p (k n) -> p k n", k=KC)
        wq = sb("wq", [P, KC, D], BF16)
        ident = sb("ident", [P, P], F32)
        ident_b = sb("ident_b", [P, P], BF16)
        slot_mask = sb("slot_mask", [P, LR], F32)
        ids0_sb = sb("ids0_sb", [1, BATCH], I32)
        ids1_sb = sb("ids1_sb", [1, BATCH], I32)
        s_in_sb = sb("s_in_sb", [P, 1], F32)
        s_w_sb = sb("s_w_sb", [P, 1], F32)
        inv_in = sb("inv_in", [P, 1], F32)
        inv_w = sb("inv_w", [P, 1], F32)
        s_out = sb("s_out", [P, 1], F32)
        ones = sb("ones", [P, 1], F32)
        x1buf = sb("x1buf", [P, 2, D], F32)
        st_h = sb("st_h", [P, D], F32R)
        st_l = sb("st_l", [P, D], F32R)
        raw = sb("raw", [P, 2, HALF], F32)
        a_raw = raw[:, :, :].rearrange("p b (j c) -> p b j c", j=PER_TILE)

        s_ids = sem("s_ids")
        s_const = sem("s_const")
        s_ident = sem("s_ident")
        mask_set = sem("mask_set")
        ones_set = sem("ones_set")
        s_scale = sem("s_scale")

        with ExitStack() as p1:
            w0h = sb("w0h", [P, KC, W0_COLS], F32R, p1)
            w0l = sb("w0l", [P, KC, W0_COLS], F32R, p1)
            b0h = sb("b0h", [P, D], F32R, p1)
            b0l = sb("b0l", [P, D], F32R, p1)
            xbuf = sb("xbuf", [P, 2, D], F32, p1)
            wbd = sb("wbd", [P, 2, P], F32, p1)
            b_base_sb = sb("b_base_sb", [P, D], F32, p1)
            hw = sb("hw", [P, ER], F32, p1)
            hwt_h = sb("hwt_h", [P, P], F32R, p1)
            hwt_l = sb("hwt_l", [P, P], F32R, p1)
            wq_val = sb("wq_val", [P, 2, HALF], F32, p1)
            wq_pow = sb("wq_pow", [P, HALF], F32, p1)
            wq_nan = wq_pow[:, :].bitcast(BF16)[:, 0:HALF]
            negmax = sb("negmax", [P, 1], F32, p1)
            esum = sb("esum", [P, 1], F32, p1)
            rsum = sb("rsum", [P, 1], F32, p1)
            top_sum = sb("top_sum", [P, 1], F32, p1)
            top_inv = sb("top_inv", [P, 1], F32, p1)
            expo = sb("expo", [P, EXPERTS], F32, p1)
            probs = sb("probs", [P, 2 * EXPERTS], F32, p1)
            sorted8 = sb("sorted8", [P, 8], F32, p1)
            to_replace = sb("to_replace", [P, 8], F32, p1)
            without_top = sb("without_top", [P, 2 * EXPERTS], F32, p1)
            top_probs = sb("top_probs", [P, EXPERTS], F32, p1)

            wq_raw = wq[:, :, :].rearrange("p k n -> p (k n)").bitcast(F32).rearrange("p (q n) -> p q n", n=HALF)
            stage = [wq_raw[:, q, :] for q in range(KC)]
            stage += [x1buf[:, q // 2, (q % 2) * HALF:(q % 2 + 1) * HALF] for q in range(4)]
            slots = len(stage)

            x_loaded = [sem(f"x_loaded{b}") for b in range(2)]
            wc_loaded = [sem(f"wc_loaded{b}") for b in range(2)]
            stage_loaded = [sem(f"stage_loaded{q}") for q in range(slots)]
            w0_hi = sem("w0_hi")
            w0_lo = sem("w0_lo")
            b_base_loaded = sem("b_base_loaded")
            wbd_zeroed = sem("wbd_zeroed")
            st_ps = [sem(f"st_ps{h}") for h in range(2)]
            hi_done = [sem(f"hi_done{h}") for h in range(2)]
            lo_done = [sem(f"lo_done{h}") for h in range(2)]
            h_ps = sem("h_ps")
            negmax_done = sem("negmax_done")
            exp_done = sem("exp_done")
            rsum_done = sem("rsum_done")
            probs_done = sem("probs_done")
            sorted_done = sem("sorted_done")
            replace_done = sem("replace_done")
            top_sum_done = sem("top_sum_done")
            top_inv_done = sem("top_inv_done")
            without_done = sem("without_done")
            top_done = sem("top_done")
            hw_done = sem("hw_done")
            hwt_ps = sem("hwt_ps")
            hwth_done = sem("hwth_done")
            hwtl_done = sem("hwtl_done")
            acc_ps = [sem(f"acc_ps{g}") for g in range(3)]
            xb_done = sem("xb_done")
            x1_done = [sem(f"x1_done{g}") for g in range(3)]
            x1_stored = [sem(f"x1_stored{b}") for b in range(2)]
            pool_loaded = [sem(f"pool_loaded{b}") for b in range(2)]
            pool_hi = sem("pool_hi")
            pool_lo = sem("pool_lo")
            split_stored = sem("split_stored")
            wq_loaded = [sem(f"wq_loaded{b}") for b in range(2)]
            wq_step = sem("wq_step")

            w0_units = [("w", g, k) for g in range(2) for k in range(KC)]
            w0_units += [("b", h, 0) for h in range(2)]
            w0_units += [("w", 2, k) for k in range(KC)]
            w0_need = (KC, 2 * KC, len(w0_units))

            def w0_places(unit):
                kind, g, k = unit
                if kind == "b":
                    cols = slice(g * HALF, (g + 1) * HALF)
                    return b0[:, cols], HALF, b0h[:, cols], b0l[:, cols]
                cols = slice(G0_START[g], G0_START[g] + G0_WIDTH[g])
                return m0[k * P:(k + 1) * P, cols], G0_WIDTH[g], w0h[:, k, cols], w0l[:, k, cols]

            pool_units = [("A", u, 0) for u in range(LORAS // 4)]
            pool_units += [("B", r, h) for r in range(LORAS * RANK // P) for h in range(2)]
            tables = len(pool_units)
            pool_units += [("W", k, g) for k in range(KC) for g in range(3)]

            def pool_places(n):
                kind, u, v = pool_units[n]
                if kind == "A":
                    src = a1[4 * u:4 * u + 4].rearrange("i p c -> p i c")
                    to = [a1_dram[4 * u:4 * u + 4, :, s * P:(s + 1) * P].rearrange("i p c -> p i c") for s in range(2)]
                elif kind == "B":
                    src = b1[u * P:(u + 1) * P, v * HALF:(v + 1) * HALF]
                    to = [b1_dram[u * P:(u + 1) * P, s, v * HALF:(v + 1) * HALF] for s in range(2)]
                else:
                    cols = slice(G1_AT[v], G1_AT[v] + G1_BASE[v])
                    src = w1t[u * P:(u + 1) * P, G1_COL[v]:G1_COL[v] + G1_BASE[v]]
                    return src, G1_BASE[v], w1h_k[:, u, cols], w1l_k[:, u, cols], None
                cols = slice(n * HALF, (n + 1) * HALF)
                return src, HALF, w1h[:, cols], w1l[:, cols], to

            def pool_pieces(t):
                return range(POOL_PIECES_A_TILE * t, min(POOL_PIECES_A_TILE * (t + 1), len(pool_units)))

            def wq_cols(u):
                return slice((u % 2) * HALF, (u % 2 + 1) * HALF)

        with ExitStack() as p2:
            obuf = sb("obuf", [P, 2, D], F32, p2)
            b_stack = [sb(f"b_stack{b}", [STACK, D], F32R, p2) for b in range(2)]
            h_masked = sb("h_masked", [P, LR], F32, p2)
            h_stack = sb("h_stack", [P, STACK], F32, p2)
            ht = sb("ht", [STACK, P], F32R, p2)
            val = sb("val", [P, D], F32, p2)
            power = sb("power", [P, D], F32, p2)
            rounded = sb("rounded", [P, D], BF16, p2)
            nan_or_0 = sb("nan_or_0", [P, D], BF16, p2)
            rq = sb("rq", [P, D], BF16, p2)
            rqt = sb("rqt", [P, D], BF16, p2)
            bias2_sb = sb("bias2_sb", [P, D], F32, p2)
            bias_raw = sb("bias_raw", [1, D], F32, p2)
            bias_h = sb("bias_h", [1, D], F32R, p2)
            bias_l = sb("bias_l", [1, D], F32R, p2)

            x1_loaded = [sem(f"x1_loaded{b}") for b in range(2)]
            a_loaded = [sem(f"a_loaded{b}") for b in range(2)]
            b_loaded = [sem(f"b_loaded{b}") for b in range(2)]
            slot_done = sem("slot_done")
            bias2_loaded = sem("bias2_loaded")
            bias_loaded = sem("bias_loaded")
            bias_split = sem("bias_split")
            bias_rows = sem("bias_rows")
            h1_ps = sem("h1_ps")
            masked_done = sem("masked_done")
            h_hi_done = sem("h_hi_done")
            h_ones = sem("h_ones")
            stack_done = sem("stack_done")
            ht_ps = sem("ht_ps")
            ht_done = sem("ht_done")
            r_ps = [sem(f"r_ps{g}") for g in range(3)]
            val_done = [sem(f"val_done{g}") for g in range(3)]
            power_done = sem("power_done")
            scaled_done = sem("scaled_done")
            shifted_done = sem("shifted_done")
            rounded_done = sem("rounded_done")
            nan_done = sem("nan_done")
            rq_done = sem("rq_done")
            rqt_ps = sem("rqt_ps")
            rqt_done = sem("rqt_done")
            f_ps = [sem(f"f_ps{h}") for h in range(2)]
            x1b_done = sem("x1b_done")
            out_done = [sem(f"out_done{h}") for h in range(2)]
            out_stored = [sem(f"out_stored{b}") for b in range(2)]

        with nc.Block() as block:

            @block.sync
            def _(sp):
                sp.dma_start(ids0_sb[:, :], ids0.rearrange("(a n) -> a n", a=1)).then_inc(s_ids, 16)
                sp.dma_start(xbuf[:, 0, :], x_t[0]).then_inc(x_loaded[0], 16)
                sp.wait_ge(s_ids, 16)
                sp.wait_ge(wbd_zeroed, 1)

                def load_cond(t, b):
                    for j in range(PER_TILE):
                        which = sp.value_load(ids0_sb[0:1, bass.ds(PER_TILE * t + j, 1)], min_val=0, max_val=15)
                        rows = slice(j * CH, (j + 1) * CH)
                        sp.dma_start(wbd[rows, b, rows],
                                     wc[bass.ds(which, 1)].rearrange("a c d -> (a c) d")).then_inc(wc_loaded[b], 16)

                load_cond(0, 0)
                for n, unit in enumerate(w0_units):
                    src, width, _, _ = w0_places(unit)
                    if n >= slots:
                        sp.wait_ge(w0_lo, n - slots + 1)
                    sp.dma_start(stage[n % slots][:, 0:width], src).then_inc(stage_loaded[n % slots], 16)
                    if n == KC - 1:
                        sp.dma_start(b_base_sb[:, :], b_base.partition_broadcast(P)).then_inc(b_base_loaded, 16)
                        sp.dma_start(s_in_sb[:, :], s_in.partition_broadcast(P)).then_inc(s_const, 16)
                        sp.dma_start(s_w_sb[:, :], s_w.partition_broadcast(P)).then_inc(s_const, 16)
                        sp.dma_start(xbuf[:, 1, :], x_t[1]).then_inc(x_loaded[1], 16)
                        load_cond(1, 1)
                sp.dma_start(ids1_sb[:, :], ids1.rearrange("(a n) -> a n", a=1)).then_inc(s_ids, 16)

                def load_pool_piece(n):
                    src, width, _, _, _ = pool_places(n)
                    sp.dma_start(raw[:, n % 2, 0:width], src).then_inc(pool_loaded[n % 2], 16)

                def load_wq_piece(u):
                    sp.dma_start(wq_val[:, u % 2, :], wf[u // 2 * P:(u // 2 + 1) * P, wq_cols(u)])\
                      .then_inc(wq_loaded[u % 2], 16)

                for n in range(2):
                    load_pool_piece(n)
                    load_wq_piece(n)

                def feed(t):
                    for n in pool_pieces(t):
                        sp.wait_ge(pool_lo, n + 1)
                        kind = pool_units[n][0]
                        _, _, hi, lo, to = pool_places(n)
                        if to:
                            for dram, part in zip(to, (hi.bitcast(F32), lo.bitcast(F32))):
                                if kind == "A":
                                    part = part.rearrange("p (i c) -> p i c", i=4)
                                sp.dma_start(dram, part).then_inc(split_stored, 16)
                        if n + 2 < len(pool_units):
                            load_pool_piece(n + 2)
                    for u in wq_pieces(t):
                        if u + 2 < 2 * KC:
                            sp.wait_ge(wq_step, WQ_STEPS * (u + 1))
                            load_wq_piece(u + 2)

                def tile(t, b):
                    sp.wait_ge(x1_done[2], t + 1)
                    sp.dma_start(x1_dram[bass.ds(t, 1)].rearrange("a p n -> (a p) n"),
                                 x1buf[:, b, :]).then_inc(x1_stored[b], 16)
                    sp.dma_start(xbuf[:, b, :], x_t[bass.ds(t + 2, 1)].rearrange("a p n -> (a p) n"))\
                      .then_inc(x_loaded[b], 16)
                    load_cond(t + 2, b)

                for t in range(PREP_TILES):
                    feed(t)
                    tile(t, t % 2)
                with sp.Fori(PREP_TILES, TILES - 3, 2) as i:
                    tile(i, 0)
                    tile(i + 1, 1)

                def load_x1(row, b):
                    sp.dma_start(x1buf[:, b, :], x1_dram[bass.ds(row, 1)].rearrange("a p n -> (a p) n"))\
                      .then_inc(x1_loaded[b], 16)

                def adapter(row, j):
                    return sp.value_load(ids1_sb[0:1, bass.ds(PER_TILE * row + j, 1)], min_val=0, max_val=LORAS - 1)

                def load_a(which, b, j):
                    sp.dma_start(a_raw[:, b, j, :], a1_dram[bass.ds(which, 1)].rearrange("a p c -> (a p) c"))\
                      .then_inc(a_loaded[b], 16)

                def load_b(which, b, j):
                    for s, part in enumerate((0, 0, 1)):
                        row = s * LR + j * RANK
                        sp.dma_start(b_stack[b][row:row + RANK, :].bitcast(F32),
                                     b1_ids[bass.ds(which, 1), :, part, :].rearrange("a r n -> (a r) n"))\
                          .then_inc(b_loaded[b], 16)

                sp.wait_ge(s_ids, 32)
                sp.wait_ge(split_stored, 32 * tables)
                sp.wait_ge(pool_lo, len(pool_units))
                for t in range(2):
                    for j in range(PER_TILE):
                        load_a(adapter(row_of(t), j), t, j)
                sp.wait_ge(x1_done[2], TILES)
                sp.dma_start(bias_raw[:, :], base_bias.rearrange("(a n) -> a n", a=1)).then_inc(bias_loaded, 16)
                for j in range(PER_TILE):
                    load_b(adapter(row_of(0), j), 0, j)
                sp.dma_start(bias2_sb[:, :], bias2.partition_broadcast(P)).then_inc(bias2_loaded, 16)
                for b in range(2):
                    sp.wait_ge(x1_stored[b], 16 * (TILES // 2 - 1))
                sp.wait_ge(bias_split, 2)
                for b in range(2):
                    for s, part in enumerate((bias_h, bias_l)):
                        sp.dma_start(b_stack[b][3 * LR + s:3 * LR + s + 1, :].bitcast(F32),
                                     part[:, :].bitcast(F32)).then_inc(bias_rows, 16)

                def store_out(t, b, row):
                    sp.wait_ge(out_done[1], t + 1)
                    sp.dma_start(out_t[bass.ds(row, 1)].rearrange("a p n -> (a p) n"), obuf[:, b, :])\
                      .then_inc(out_stored[b], 16)

                def tile(t, b, adapters, stored):
                    if adapters is not None:
                        first = isinstance(t, int) and t == 0
                        if not first:
                            sp.wait_ge(r_ps[2], t)
                            sp.wait_ge(slot_done, t)
                        for j in range(PER_TILE):
                            which = adapter(adapters, j)
                            if not first:
                                load_a(which, 1 - b, j)
                            load_b(which, 1 - b, j)
                    if stored is not None:
                        store_out(t - 2, b, stored)
                    if adapters is not None and (not isinstance(t, int) or t < TILES - 2):
                        sp.wait_ge(h1_ps, t + 1)
                        sp.wait_ge(x1b_done, t + 1)
                        load_x1(t, b)

                for t in range(4):
                    tile(t, t % 2, row_of(t + 1), row_of(t - 2) if t >= 2 else None)
                with sp.Fori(4, TILES - 3, 2) as i:
                    tile(i, 0, i - 1, i - 4)
                    tile(i + 1, 1, i, i - 3)
                tile(TILES - 2, 0, row_of(TILES - 1), row_of(TILES - 4))
                tile(TILES - 1, 1, None, row_of(TILES - 3))
                store_out(TILES - 2, 0, row_of(TILES - 2))
                store_out(TILES - 1, 1, row_of(TILES - 1))
                for b in range(2):
                    sp.wait_ge(out_stored[b], 16 * TILES // 2)

            @block.gpsimd
            def _(pool):
                pool.memset(wbd[:, :, :], 0.0).then_inc(wbd_zeroed, 1)
                pool.memset(ones[:, :], 1.0).then_inc(ones_set, 1)
                pool.memset(ident[:, :], 0.0).then_inc(s_ident, 1)
                pool.memset(ident_b[:, :], 0.0).then_inc(s_ident, 1)
                pool.wait_ge(s_ident, 2)
                for m in (ident, ident_b):
                    pool.affine_select(out=m[:, :], in_=m[:, :], compare_op=ALU.not_equal, fill=1.0, base=0,
                                       pattern=[[-1, P]], channel_multiplier=1).then_inc(s_ident, 1)
                pool.wait_ge(b_base_loaded, 16)

                def add_bias(t, b):
                    pool.wait_ge(st_ps[1], t + 1)
                    pool.tensor_tensor(xbuf[:, b, :], xbuf[:, b, :], b_base_sb[:, :], ALU.add).then_inc(xb_done, 1)

                def split(n):
                    _, width, hi, lo, _ = pool_places(n)
                    piece = raw[:, n % 2, 0:width]
                    pool.wait_ge(pool_loaded[n % 2], 16 * (n // 2 + 1))
                    if n == tables:
                        pool.wait_ge(split_stored, 32 * tables)
                    pool.tensor_scalar(hi, piece, 1.0, None, ALU.mult).then_inc(pool_hi, 1)
                    pool.wait_ge(pool_hi, n + 1)
                    pool.tensor_tensor(lo, piece, hi, ALU.subtract).then_inc(pool_lo, 1)

                for t in range(PREP_TILES):
                    add_bias(t, t % 2)
                    for n in pool_pieces(t):
                        split(n)
                with pool.Fori(PREP_TILES, TILES - 1, 2) as i:
                    add_bias(i, 0)
                    add_bias(i + 1, 1)

                one = ones[:, :].unsqueeze(2)

                def fill_slot(t, b, loads, lag):
                    pool.wait_ge(a_loaded[b], 32 * loads)
                    if lag:
                        pool.wait_ge(h1_ps, t - 1)
                    at = b * (LR + G1_BASE[0])
                    for s, w in enumerate((w1h_k, w1l_k)):
                        to = w[:, :, at:at + LR].rearrange("p k (j r) -> p j k r", j=PER_TILE)
                        for j in range(PER_TILE):
                            part = a_raw[:, b, j, s * P:(s + 1) * P].rearrange("p (k r) -> p k r", r=RANK)
                            last = pool.tensor_tensor(to[:, j], part, one.to_broadcast([P, KC, RANK]), ALU.mult)
                    last.then_inc(slot_done, 1)

                pool.wait_ge(ones_set, 1)
                fill_slot(0, 0, 1, False)
                pool.wait_ge(x1_done[2], TILES)
                pool.memset(h_stack[:, :], 1.0).then_inc(h_ones, 1)
                pool.wait_ge(bias2_loaded, 16)

                def tile(t, b, x1_loads, a_loads, stored, lag):
                    if x1_loads is not None:
                        pool.wait_ge(x1_loaded[b], 16 * x1_loads)
                    if stored is not None:
                        pool.wait_ge(out_stored[b], stored)
                    pool.tensor_tensor(obuf[:, b, :], x1buf[:, b, :], bias2_sb[:, :], ALU.add).then_inc(x1b_done, 1)
                    if a_loads is not None:
                        fill_slot(t + 1, 1 - b, a_loads, lag)

                tile(0, 0, None, 1, None, False)
                tile(1, 1, None, 2, None, True)
                with pool.Fori(2, TILES - 3, 2) as i:
                    half = pool.snap(i // 2)
                    tile(i, 0, half, half + 1, 8 * i, True)
                    tile(i + 1, 1, half, half + 2, 8 * i, True)
                tile(TILES - 2, 0, TILES // 2 - 1, TILES // 2, 8 * (TILES - 2), True)
                tile(TILES - 1, 1, TILES // 2 - 1, None, 8 * (TILES - 2), True)

            @block.scalar
            def _(act):
                def st_hi(t):
                    for h in range(2):
                        act.wait_ge(st_ps[h], t + 1)
                        act.activation(st_h[:, h * HALF:(h + 1) * HALF], bank_t[:, h, :], ACT.Copy)\
                           .then_inc(hi_done[h], 1)

                for n, unit in enumerate(w0_units):
                    _, width, hi, _ = w0_places(unit)
                    act.wait_ge(stage_loaded[n % slots], 16 * (n // slots + 1))
                    act.activation(hi, stage[n % slots][:, 0:width], ACT.Copy,
                                   scale=LORA_SCALE if unit[0] == "b" else 1.0).then_inc(w0_hi, 1)
                    if n == 1:
                        st_hi(0)

                def tile(t, more):
                    act.wait_ge(negmax_done, t + 1)
                    act.activation(expo[:, :], bank_g[:, 0, ER:ER + EXPERTS], ACT.Exp, bias=negmax[:, :],
                                   accum_out=esum[:, :]).then_inc(exp_done, 1)
                    act.wait_ge(hwt_ps, t + 1)
                    act.activation(hwt_h[:, :], bank_m[:, 0:P], ACT.Copy).then_inc(hwth_done, 1)
                    if more:
                        st_hi(t + 1)

                tile(0, True)
                tile(1, True)
                with act.Fori(2, TILES - 3, 2) as i:
                    tile(i, True)
                    tile(i + 1, True)
                tile(TILES - 2, True)
                tile(TILES - 1, True)

                act.wait_ge(x1_done[2], TILES)
                act.wait_ge(bias_loaded, 16)
                act.activation(bias_h[:, :], bias_raw[:, :], ACT.Copy).then_inc(bias_split, 1)

                def rq_out(t):
                    act.wait_ge(rqt_ps, t + 1)
                    act.activation(rqt[:, :], rq_ps, ACT.Copy).then_inc(rqt_done, 1)

                def tile(t, b, lag, more):
                    act.wait_ge(ht_ps, t + 1)
                    act.activation(ht[:, :], bank_f[0:STACK, 0, 0:P], ACT.Copy).then_inc(ht_done, 1)
                    if lag:
                        rq_out(t - 1)
                    if more:
                        st_hi(TILES + t + 1)
                    if lag:
                        act.wait_ge(rounded_done, t)
                    for g in range(3):
                        act.wait_ge(r_ps[g], t + 1)
                        at = LR if g == 0 and b == 0 else 0
                        act.activation(val[:, G1_COL[g]:G1_COL[g] + G1_BASE[g]],
                                       bank_g[:, g, at:at + G1_BASE[g]], ACT.Copy, scale=inv_in[:, :])\
                           .then_inc(val_done[g], 1)

                tile(0, 0, False, True)
                tile(1, 1, True, True)
                with act.Fori(2, TILES - 3, 2) as i:
                    tile(i, 0, True, True)
                    tile(i + 1, 1, True, True)
                tile(TILES - 2, 0, True, True)
                tile(TILES - 1, 1, True, False)
                rq_out(TILES - 1)

            @block.vector
            def _(dve):
                dve.memset(probs[:, :], -1.0).then_inc(probs_done, 1)
                dve.memset(to_replace[:, :], -1.0).then_inc(replace_done, 1)
                dve.memset(slot_mask[:, :], 0.0).then_inc(mask_set, 1)
                dve.wait_ge(mask_set, 1)
                for j in range(PER_TILE):
                    dve.memset(slot_mask[j * CH:(j + 1) * CH, j * RANK:(j + 1) * RANK], 1.0).then_inc(mask_set, 1)

                def st_lo(t, h):
                    half = slice(h * HALF, (h + 1) * HALF)
                    dve.wait_ge(hi_done[h], t + 1)
                    dve.tensor_tensor(st_l[:, half], bank_t[:, h, :], st_h[:, half], ALU.subtract)\
                       .then_inc(lo_done[h], 1)

                for n, unit in enumerate(w0_units):
                    _, width, hi, lo = w0_places(unit)
                    dve.wait_ge(w0_hi, n + 1)
                    piece = stage[n % slots][:, 0:width]
                    if unit[0] == "b":
                        dve.scalar_tensor_tensor(lo, piece, LORA_SCALE, hi, ALU.mult, ALU.subtract).then_inc(w0_lo, 1)
                    else:
                        dve.tensor_tensor(lo, piece, hi, ALU.subtract).then_inc(w0_lo, 1)
                    if n == 1:
                        st_lo(0, 0)
                        st_lo(0, 1)
                dve.wait_ge(s_const, 32)
                dve.reciprocal(inv_in[:, :], s_in_sb[:, :]).then_inc(s_scale, 1)
                dve.reciprocal(inv_w[:, :], s_w_sb[:, :]).then_inc(s_scale, 1)
                dve.tensor_tensor(s_out[:, :], s_in_sb[:, :], s_w_sb[:, :], ALU.mult).then_inc(s_scale, 1)
                dve.wait_ge(s_scale, 3)

                def quantize_weight(u):
                    val = wq_val[:, u % 2, :]
                    power = wq_pow[:, :]
                    to = wq[:, u // 2, wq_cols(u)]
                    base = WQ_STEPS * u
                    dve.wait_ge(wq_loaded[u % 2], 16 * (u // 2 + 1))
                    dve.tensor_scalar(val, val, inv_w[:, :], None, ALU.mult).then_inc(wq_step, 1)
                    dve.wait_ge(wq_step, base + 1)
                    dve.tensor_scalar(power.bitcast(U32), val.bitcast(U32), 0x7F800000, None, ALU.bitwise_and)\
                       .then_inc(wq_step, 1)
                    dve.wait_ge(wq_step, base + 2)
                    dve.tensor_scalar(power, power, MIN_NORMAL, ROUND_C, ALU.max, ALU.mult).then_inc(wq_step, 1)
                    dve.wait_ge(wq_step, base + 3)
                    dve.tensor_tensor(val, val, power, ALU.add).then_inc(wq_step, 1)
                    dve.wait_ge(wq_step, base + 4)
                    dve.tensor_tensor(to, val, power, ALU.subtract).then_inc(wq_step, 1)
                    dve.wait_ge(wq_step, base + 5)
                    dve.tensor_scalar(wq_nan, to, OVERFLOW_C, 0.0, ALU.mult, ALU.mult).then_inc(wq_step, 1)
                    dve.wait_ge(wq_step, base + 6)
                    dve.tensor_tensor(to, to, wq_nan, ALU.add).then_inc(wq_step, 1)

                def tile(t, b, stored, wq_units=()):
                    n = t + 1
                    dve.wait_ge(h_ps, n)
                    dve.tensor_reduce(negmax[:, :], bank_g[:, 0, ER:ER + EXPERTS], AXIS.X, ALU.max, negate=True)\
                       .then_inc(negmax_done, 1)
                    dve.wait_ge(exp_done, n)
                    dve.reciprocal(rsum[:, :], esum[:, :]).then_inc(rsum_done, 1)
                    dve.max(sorted8[:, :], expo[:, :]).then_inc(sorted_done, 1)
                    dve.wait_ge(rsum_done, n)
                    dve.tensor_scalar(probs[:, 0:EXPERTS], expo[:, :], rsum[:, :], None, ALU.mult)\
                       .then_inc(probs_done, 1)
                    dve.wait_ge(sorted_done, n)
                    dve.tensor_scalar(to_replace[:, 0:2], sorted8[:, 0:2], rsum[:, :], None, ALU.mult)\
                       .then_inc(replace_done, 1)
                    dve.wait_ge(probs_done, n + 1)
                    dve.wait_ge(replace_done, n + 1)
                    dve.tensor_tensor(top_sum[:, :], to_replace[:, 0:1], to_replace[:, 1:2], ALU.add)\
                       .then_inc(top_sum_done, 1)
                    dve.match_replace(without_top[:, :], to_replace[:, :], probs[:, :], 0.0)\
                       .then_inc(without_done, 1)
                    dve.wait_ge(top_sum_done, n)
                    dve.reciprocal(top_inv[:, :], top_sum[:, :]).then_inc(top_inv_done, 1)
                    dve.wait_ge(without_done, n)
                    dve.tensor_tensor(top_probs[:, :], probs[:, 0:EXPERTS], without_top[:, 0:EXPERTS],
                                      ALU.subtract).then_inc(top_done, 1)
                    dve.wait_ge(top_done, n)
                    dve.wait_ge(top_inv_done, n)
                    gate = top_probs[:, :].unsqueeze(2).to_broadcast([P, EXPERTS, RANK])
                    dve.scalar_tensor_tensor(hw[:, :].rearrange("p (e r) -> p e r", r=RANK),
                                             bank_g[:, 0, 0:ER].rearrange("p (e r) -> p e r", r=RANK),
                                             top_inv[:, :], gate, ALU.mult, ALU.mult).then_inc(hw_done, 1)
                    for u in wq_units[0:1]:
                        quantize_weight(u)
                    dve.wait_ge(hwth_done, n)
                    dve.tensor_tensor(hwt_l[:, :], bank_m[:, 0:P], hwt_h[:, :], ALU.subtract).then_inc(hwtl_done, 1)
                    for u in wq_units[1:2]:
                        quantize_weight(u)
                    st_lo(n, 0)
                    dve.wait_ge(xb_done, n)
                    if stored is not None:
                        dve.wait_ge(x1_stored[b], stored)
                    for g in range(3):
                        dve.wait_ge(acc_ps[g], n)
                        width = G0_WIDTH[g] - G0_OUT[g]
                        cols = slice(G0_COL[g], G0_COL[g] + width)
                        dve.tensor_tensor(x1buf[:, b, cols], bank_g[:, g, G0_OUT[g]:G0_WIDTH[g]],
                                          xbuf[:, b, cols], ALU.add).then_inc(x1_done[g], 1)
                        if g == 0:
                            st_lo(n, 1)

                for t in range(PREP_TILES):
                    tile(t, t % 2, 16 * (t // 2) if t >= 2 else None, wq_pieces(t))
                with dve.Fori(PREP_TILES, TILES - 1, 2) as i:
                    tile(i, 0, 8 * i)
                    tile(i + 1, 1, 8 * i)

                def quantize(t):
                    n = t + 1
                    dve.wait_ge(val_done[2], n)
                    dve.tensor_scalar(power[:, :].bitcast(U32), val[:, :].bitcast(U32), 0x7F800000, None,
                                      ALU.bitwise_and).then_inc(power_done, 1)
                    dve.wait_ge(power_done, n)
                    dve.tensor_scalar(power[:, :], power[:, :], MIN_NORMAL, ROUND_C, ALU.max, ALU.mult)\
                       .then_inc(scaled_done, 1)
                    dve.wait_ge(scaled_done, n)
                    dve.tensor_tensor(val[:, :], val[:, :], power[:, :], ALU.add).then_inc(shifted_done, 1)
                    dve.wait_ge(shifted_done, n)
                    dve.tensor_tensor(rounded[:, :], val[:, :], power[:, :], ALU.subtract)\
                       .then_inc(rounded_done, 1)
                    dve.wait_ge(rounded_done, n)
                    dve.tensor_scalar(nan_or_0[:, :], rounded[:, :], OVERFLOW_C, 0.0, ALU.mult, ALU.mult)\
                       .then_inc(nan_done, 1)
                    dve.wait_ge(nan_done, n)
                    dve.tensor_tensor(rq[:, :], rounded[:, :], nan_or_0[:, :], ALU.add).then_inc(rq_done, 1)

                def finish(t, b):
                    dve.wait_ge(x1b_done, t + 1)
                    for h in range(2):
                        half = slice(h * HALF, (h + 1) * HALF)
                        dve.wait_ge(f_ps[h], t + 1)
                        dve.scalar_tensor_tensor(obuf[:, b, half], bank_f[:, h, :], s_out[:, :],
                                                 obuf[:, b, half], ALU.mult, ALU.add).then_inc(out_done[h], 1)

                def stack_h(t, b):
                    n = t + 1
                    at = 0 if b == 0 else G1_BASE[0]
                    dve.wait_ge(h1_ps, n)
                    dve.tensor_tensor(h_masked[:, :], bank_g[:, 0, at:at + LR], slot_mask[:, :], ALU.mult)\
                       .then_inc(masked_done, 1)
                    dve.wait_ge(masked_done, n)
                    for s in (0, 2):
                        last = dve.tensor_copy(h_stack[:, s * LR:(s + 1) * LR].bitcast(F32R), h_masked[:, :])
                    last.then_inc(h_hi_done, 1)
                    dve.wait_ge(h_hi_done, n)
                    dve.tensor_tensor(h_stack[:, LR:2 * LR], h_masked[:, :], h_stack[:, 0:LR], ALU.subtract)\
                       .then_inc(stack_done, 1)

                def tile(t, b, lag, more):
                    if lag >= 1:
                        quantize(t - 1)
                    if lag >= 2:
                        finish(t - 2, b)
                    stack_h(t, b)
                    if more:
                        st_lo(TILES + t + 1, 0)
                        st_lo(TILES + t + 1, 1)

                dve.wait_ge(bias_split, 1)
                dve.tensor_tensor(bias_l[:, :], bias_raw[:, :], bias_h[:, :], ALU.subtract).then_inc(bias_split, 1)
                dve.wait_ge(h_ones, 1)
                tile(0, 0, 0, True)
                tile(1, 1, 1, True)
                with dve.Fori(2, TILES - 3, 2) as i:
                    tile(i, 0, 2, True)
                    tile(i + 1, 1, 2, True)
                tile(TILES - 2, 0, 2, True)
                tile(TILES - 1, 1, 2, False)
                quantize(TILES - 1)
                finish(TILES - 2, 0)
                finish(TILES - 1, 1)

            @block.tensor
            def _(pe):
                def cond(t, b, loads):
                    pe.wait_ge(x_loaded[b], 16 * loads)
                    pe.wait_ge(wc_loaded[b], 32 * loads)
                    for k in range(KC):
                        cols = slice((k % 4) * P, (k % 4 + 1) * P)
                        last = pe.matmul(bank_t[:, k // 4, cols], xbuf[:, b, k * P:(k + 1) * P], wbd[:, b, :],
                                         start=True, stop=True)
                        if k % 4 == 3:
                            last.then_inc(st_ps[k // 4], 1)

                def bank(g, n):
                    cols = slice(G0_START[g], G0_START[g] + G0_WIDTH[g])
                    to = bank_g[:, g, 0:G0_WIDTH[g]]
                    for k in range(KC):
                        if g == 0 and k == KC // 2:
                            pe.wait_ge(lo_done[1], n)
                        rows = slice(k * P, (k + 1) * P)
                        pe.matmul(to, st_h[:, rows], w0h[:, k, cols], start=(k == 0), stop=False)
                        pe.matmul(to, st_h[:, rows], w0l[:, k, cols], start=False, stop=False)
                        last = pe.matmul(to, st_l[:, rows], w0h[:, k, cols], start=False, stop=(k == KC - 1))
                    return last

                def tile(t, b, loads, prior, more):
                    n = t + 1
                    pe.wait_ge(lo_done[0], n)
                    for g in range(3):
                        if prior:
                            pe.wait_ge(x1_done[g], t)
                        else:
                            pe.wait_ge(w0_lo, w0_need[g])
                        last = bank(g, n)
                        if g == 0:
                            last.then_inc(h_ps, 1)
                        if g == 1:
                            pe.wait_ge(hw_done, n)
                            pe.transpose(bank_m[:, 0:P], hw[:, :], ident[:, :]).then_inc(hwt_ps, 1)
                    if more:
                        cond(n, 1 - b, loads)
                    else:
                        transpose_x(0, 0, None)
                    pe.wait_ge(hwtl_done, n)
                    for g in range(3):
                        to = bank_g[:, g, G0_OUT[g]:G0_WIDTH[g]]
                        cols = slice(G0_COL[g], G0_COL[g] + G0_WIDTH[g] - G0_OUT[g])
                        pe.matmul(to, hwt_h[:, :], b0h[:, cols], start=False, stop=False, skip_group_check=True)
                        pe.matmul(to, hwt_h[:, :], b0l[:, cols], start=False, stop=False, skip_group_check=True)
                        pe.matmul(to, hwt_l[:, :], b0h[:, cols], start=False, stop=True, skip_group_check=True)\
                          .then_inc(acc_ps[g], 1)

                def transpose_x(t, b, loads):
                    if loads is not None:
                        pe.wait_ge(x1_loaded[b], 16 * loads)
                    else:
                        pe.wait_ge(x1_done[2], TILES - 1 + t)
                    for k in range(KC):
                        cols = slice((k % 4) * P, (k % 4 + 1) * P)
                        last = pe.transpose(bank_t[:, k // 4, cols], x1buf[:, b, k * P:(k + 1) * P], ident[:, :])
                        if k % 4 == 3:
                            last.then_inc(st_ps[k // 4], 1)

                pe.wait_ge(s_ident, 4)
                cond(0, 0, 1)
                tile(0, 0, 1, False, True)
                tile(1, 1, 2, True, True)
                with pe.Fori(2, TILES - 3, 2) as i:
                    half = pe.snap(i // 2)
                    tile(i, 0, half + 1, True, True)
                    tile(i + 1, 1, half + 2, True, True)
                tile(TILES - 2, 0, TILES // 2, True, True)
                tile(TILES - 1, 1, None, True, False)

                def bank(g, b, n):
                    if g == 0:
                        cols = slice(b * LR, b * LR + LR + G1_BASE[0])
                    else:
                        cols = slice(G1_AT[g], G1_AT[g] + G1_BASE[g])
                    to = bank_g[:, g, 0:cols.stop - cols.start]
                    for k in range(KC):
                        if g == 0 and k == KC // 2:
                            pe.wait_ge(lo_done[1], TILES + n)
                        rows = slice(k * P, (k + 1) * P)
                        pe.matmul(to, st_h[:, rows], w1h_k[:, k, cols], start=(k == 0), stop=False)
                        pe.matmul(to, st_h[:, rows], w1l_k[:, k, cols], start=False, stop=False)
                        last = pe.matmul(to, st_l[:, rows], w1h_k[:, k, cols], start=False, stop=(k == KC - 1))
                    return last

                def transpose_rq(t):
                    pe.wait_ge(rq_done, t + 1)
                    for k in range(KC):
                        rows = slice(k * P, (k + 1) * P)
                        last = pe.transpose(rq_ps[:, rows], rq[:, rows], ident_b[:, :])
                    last.then_inc(rqt_ps, 1)

                def ffn(t):
                    pe.wait_ge(rqt_done, t + 1)
                    for h in range(2):
                        for k in range(KC):
                            last = pe.matmul(bank_f[:, h, :], rqt[:, k * P:(k + 1) * P],
                                             wq[:, k, h * HALF:(h + 1) * HALF], start=(k == 0), stop=(k == KC - 1))
                        last.then_inc(f_ps[h], 1)

                def tile(t, b, loads, x1_loads, lag, more):
                    n = t + 1
                    pe.wait_ge(lo_done[0], TILES + n)
                    pe.wait_ge(slot_done, n)
                    for g in range(3):
                        if lag:
                            pe.wait_ge(val_done[g], t)
                        else:
                            pe.wait_ge(x1_done[g], TILES)
                        last = bank(g, b, n)
                        if g == 0:
                            last.then_inc(h1_ps, 1)
                        if g == 1:
                            if lag == 2:
                                pe.wait_ge(out_done[1], t - 1)
                            pe.wait_ge(stack_done, n)
                            pe.transpose(bank_f[0:STACK, 0, 0:P], h_stack[:, :], ident[:, :]).then_inc(ht_ps, 1)
                            if lag:
                                transpose_rq(t - 1)
                    if more:
                        transpose_x(n, 1 - b, x1_loads)
                    if not lag:
                        pe.wait_ge(bias_rows, 64)
                    pe.wait_ge(b_loaded[b], 96 * loads)
                    pe.wait_ge(ht_done, n)
                    for g in range(3):
                        at = LR if g == 0 and b == 0 else 0
                        pe.matmul(bank_g[:, g, at:at + G1_BASE[g]], ht[:, :],
                                  b_stack[b][:, G1_COL[g]:G1_COL[g] + G1_BASE[g]],
                                  start=False, stop=True, skip_group_check=True).then_inc(r_ps[g], 1)
                    if lag:
                        ffn(t - 1)

                tile(0, 0, 1, None, 0, True)
                tile(1, 1, 1, 1, 1, True)
                with pe.Fori(2, TILES - 3, 2) as i:
                    half = pe.snap(i // 2)
                    tile(i, 0, half + 1, half, 2, True)
                    tile(i + 1, 1, half + 1, half + 1, 2, True)
                tile(TILES - 2, 0, TILES // 2, TILES // 2 - 1, 2, True)
                tile(TILES - 1, 1, TILES // 2, None, 2, False)
                transpose_rq(TILES - 1)
                pe.wait_ge(out_done[1], TILES - 1)
                ffn(TILES - 1)


def kernel(x, itok_B_0_15, itok_B_6_15, L0_cond_weights, L0_ffn_W_base, L0_ffn_b_base, L0_ffn_W_router,
           L0_ffn_A, L0_ffn_B, L1_cond_base_weight, L1_cond_base_bias, L1_cond_lora_A_w, L1_cond_lora_B_w,
           L1_ffn_weight, L1_ffn_bias, L1_ffn_input_scale, L1_ffn_weight_scale):
    import concourse.bacc as bacc
    from concourse.bass_utils import run_bass_kernel_spmd

    def lay(a):
        return np.ascontiguousarray(a)

    a_w = np.asarray(L1_cond_lora_A_w)
    arrays = {
        "x": lay(x),
        "ids0": lay(itok_B_0_15),
        "ids1": lay(itok_B_6_15),
        "wc": lay(L0_cond_weights),
        "m0": lay(np.concatenate([np.asarray(L0_ffn_A).reshape(ER, D), np.asarray(L0_ffn_W_router),
                                  np.asarray(L0_ffn_W_base)]).T),
        "b0": lay(np.asarray(L0_ffn_B).transpose(0, 2, 1).reshape(ER, D)),
        "b_base": lay(L0_ffn_b_base),
        "w1t": lay(np.asarray(L1_cond_base_weight).T),
        "base_bias": lay(L1_cond_base_bias),
        "a1": lay(a_w.reshape(LORAS, RANK, KC, P).transpose(0, 3, 2, 1).reshape(LORAS, P, KC * RANK)),
        "b1": lay(np.asarray(L1_cond_lora_B_w).transpose(0, 2, 1).reshape(LORAS * RANK, D)),
        "wf": lay(L1_ffn_weight),
        "bias2": lay(L1_ffn_bias),
        "s_in": lay(L1_ffn_input_scale),
        "s_w": lay(L1_ffn_weight_scale),
    }
    nc = bacc.Bacc("TRN2", target_bir_lowering=False, num_devices=1)
    args = {n: nc.dram_tensor(n, a.shape, mybir.dt.from_np(a.dtype), kind="ExternalInput").ap()
            for n, a in arrays.items()}
    out = nc.dram_tensor("out", (BATCH, CH, D), F32, kind="ExternalOutput").ap()
    build(nc, out=out, **args)
    r = run_bass_kernel_spmd(nc, [arrays], core_ids=[0])
    return r.results[0]["out"]
```

```python
from contextlib import ExitStack
from itertools import zip_longest

import numpy as np

import concourse.bass as bass
from concourse import mybir

F32 = mybir.dt.float32
F32R = mybir.dt.float32r
BF16 = mybir.dt.bfloat16
U32 = mybir.dt.uint32
I32 = mybir.dt.int32
ALU = mybir.AluOpType
ACT = mybir.ActivationFunctionType
AXIS = mybir.AxisListType

P = 128
BATCH, CH, D = 128, 64, 1024
TILES = BATCH * CH // P
PER_TILE = P // CH
KC = D // P
HALF = 512
EXPERTS, RANK = 8, 16
ER = EXPERTS * RANK
LORA_SCALE = 2.0
LORAS = 32
LR = PER_TILE * RANK

G0_START = (0, 392, 776)
G0_WIDTH = (392, 384, 384)
G0_OUT = (ER + EXPERTS, 0, 0)
G0_COL = (0, 256, 640)
W0_COLS = ER + EXPERTS + D

G1_BASE = (320, 352, 352)
G1_COL = (0, 320, 672)
G1_AT = tuple(LR + c for c in G1_COL)
W1_COLS = LR + D
STACK = 3 * LR + 2

ROUND_C = 1.5 * 2.0 ** 20
MIN_NORMAL = 2.0 ** -6
OVERFLOW_C = float(np.float32(2.0 ** 127 / 235.0))

PREP_TILES = 18
WQ_TILES = range(2, 18)
WQ_A_TILE = 2
WQ_COLS = 256
WQ_PIECES = D * D // P // WQ_COLS
WQ_STEPS = 7
POOL_PIECES_A_TILE = 3


def wq_pieces(t):
    first = WQ_A_TILE * (t - WQ_TILES[0])
    return range(first, min(first + WQ_A_TILE, WQ_PIECES)) if t in WQ_TILES else ()


def build(nc, x, ids0, ids1, wc, m0, b0, b_base, w1t, base_bias, a1, b1, wf, bias2, s_in, s_w, out):
    x_t = x.rearrange("b c t -> (b c) t").rearrange("(n p) t -> n p t", p=P)
    out_t = out.rearrange("b c t -> (b c) t").rearrange("(n p) t -> n p t", p=P)
    x1_dram = nc.dram_tensor("x1_scratch", (TILES, P, D), F32, kind="Internal").ap()
    x1t_dram = nc.dram_tensor("x1t_scratch", (TILES, P, D), F32, kind="Internal").ap()
    a1_dram = nc.dram_tensor("a1_split", (LORAS, P, 2 * KC * RANK), F32, kind="Internal").ap()
    b1_dram = nc.dram_tensor("b1_split", (LORAS * RANK, 2, D), F32, kind="Internal").ap()
    b1_ids = b1_dram.rearrange("(i r) s n -> i r s n", r=RANK)

    with ExitStack() as whole:
        def sb(name, shape, dt, stack=whole):
            return stack.enter_context(nc.sbuf_tensor(name, shape, dt))

        def sem(name):
            return whole.enter_context(nc.semaphore(name))

        bank_g = whole.enter_context(nc.psum_tensor("bank_g", [P, 3, 512], F32))
        bank_t = whole.enter_context(nc.psum_tensor("bank_t", [P, 2, 512], F32))
        bank_f = whole.enter_context(nc.psum_tensor("bank_f", [P, 2, 512], F32))

        w1h = sb("w1h", [P, KC * W1_COLS], F32R)
        w1l = sb("w1l", [P, KC * W1_COLS], F32R)
        w1h_k = w1h[:, :].rearrange("p (k n) -> p k n", k=KC)
        w1l_k = w1l[:, :].rearrange("p (k n) -> p k n", k=KC)
        wq = sb("wq", [P, KC, D], BF16)
        slot_mask = sb("slot_mask", [P, LR], F32)
        ids0_sb = sb("ids0_sb", [1, BATCH], I32)
        ids1_sb = sb("ids1_sb", [1, BATCH], I32)
        s_in_sb = sb("s_in_sb", [P, 1], F32)
        s_w_sb = sb("s_w_sb", [P, 1], F32)
        inv_in = sb("inv_in", [P, 1], F32)
        inv_w = sb("inv_w", [P, 1], F32)
        s_out = sb("s_out", [P, 1], F32)
        ones = sb("ones", [P, 1], F32)
        xbuf = sb("xbuf", [P, 2, D], F32)
        x1buf = sb("x1buf", [P, 2, D], F32)
        st_h = sb("st_h", [P, D], F32R)
        st_l = sb("st_l", [P, D], F32R)
        raw = sb("raw", [P, 2, HALF], F32)
        a_raw = raw[:, :, :].rearrange("p b (j c) -> p b j c", j=PER_TILE)

        s_ids = sem("s_ids")
        s_const = sem("s_const")
        mask_set = sem("mask_set")
        ones_set = sem("ones_set")
        s_scale = sem("s_scale")

        with ExitStack() as p1:
            w0h = sb("w0h", [P, KC, W0_COLS], F32R, p1)
            w0l = sb("w0l", [P, KC, W0_COLS], F32R, p1)
            b0h = sb("b0h", [P, D], F32R, p1)
            b0l = sb("b0l", [P, D], F32R, p1)
            x1_blocks = sb("x1_blocks", [P, D], F32, p1)
            wbd = sb("wbd", [P, 2, P], F32, p1)
            b_base_sb = sb("b_base_sb", [P, D], F32, p1)
            hw = sb("hw", [P, ER], F32, p1)
            hw_parts = sb("hw_parts", [P, 2, ER], F32, p1)
            hwt = sb("hwt", [P, 2, P], F32R, p1)
            wq_val = sb("wq_val", [P, 2, WQ_COLS], F32, p1)
            wq_pow = sb("wq_pow", [P, WQ_COLS], F32, p1)
            wq_nan = wq_pow[:, :].bitcast(BF16)[:, 0:WQ_COLS]
            negmax = sb("negmax", [P, 1], F32, p1)
            esum = sb("esum", [P, 1], F32, p1)
            rsum = sb("rsum", [P, 1], F32, p1)
            top_sum = sb("top_sum", [P, 1], F32, p1)
            top_inv = sb("top_inv", [P, 1], F32, p1)
            expo = sb("expo", [P, EXPERTS], F32, p1)
            probs = sb("probs", [P, 2 * EXPERTS], F32, p1)
            sorted8 = sb("sorted8", [P, 8], F32, p1)
            to_replace = sb("to_replace", [P, 8], F32, p1)
            without_top = sb("without_top", [P, 2 * EXPERTS], F32, p1)
            top_probs = sb("top_probs", [P, EXPERTS], F32, p1)

            wq_raw = wq[:, :, :].rearrange("p k n -> p (k n)").bitcast(F32).rearrange("p (q n) -> p q n", n=HALF)
            stage = [wq_raw[:, q, :] for q in range(KC)]
            stage += [x1buf[:, q // 2, (q % 2) * HALF:(q % 2 + 1) * HALF] for q in range(4)]
            slots = len(stage)

            x_loaded = [sem(f"x_loaded{b}") for b in range(2)]
            wc_loaded = [sem(f"wc_loaded{b}") for b in range(2)]
            stage_loaded = [sem(f"stage_loaded{q}") for q in range(slots)]
            w0_hi = sem("w0_hi")
            w0_lo = sem("w0_lo")
            b_base_loaded = sem("b_base_loaded")
            wbd_zeroed = sem("wbd_zeroed")
            st_ps = [sem(f"st_ps{h}") for h in range(2)]
            hi_done = [sem(f"hi_done{h}") for h in range(2)]
            lo_done = [sem(f"lo_done{h}") for h in range(2)]
            h_ps = sem("h_ps")
            negmax_done = sem("negmax_done")
            exp_done = sem("exp_done")
            rsum_done = sem("rsum_done")
            probs_done = sem("probs_done")
            sorted_done = sem("sorted_done")
            replace_done = sem("replace_done")
            top_sum_done = sem("top_sum_done")
            top_inv_done = sem("top_inv_done")
            without_done = sem("without_done")
            top_done = sem("top_done")
            hw_done = sem("hw_done")
            hw_turned = sem("hw_turned")
            hw_hi_done = sem("hw_hi_done")
            hw_lo_done = sem("hw_lo_done")
            hwt_done = [sem(f"hwt_done{e}") for e in range(2)]
            acc_ps = [sem(f"acc_ps{g}") for g in range(3)]
            xb_done = sem("xb_done")
            x1_done = [sem(f"x1_done{g}") for g in range(3)]
            blocks_done = sem("blocks_done")
            blocks_stored = sem("blocks_stored")
            x1_stored = [sem(f"x1_stored{b}") for b in range(2)]
            pool_loaded = [sem(f"pool_loaded{b}") for b in range(2)]
            pool_hi = sem("pool_hi")
            pool_lo = sem("pool_lo")
            split_stored = sem("split_stored")
            wq_loaded = [sem(f"wq_loaded{b}") for b in range(2)]
            wq_step = sem("wq_step")

            w0_units = [("w", g, k) for g in range(2) for k in range(KC)]
            w0_units += [("b", h, 0) for h in range(2)]
            w0_units += [("w", 2, k) for k in range(KC)]
            w0_need = (KC, 2 * KC, len(w0_units))

            def w0_places(unit):
                kind, g, k = unit
                if kind == "b":
                    cols = slice(g * HALF, (g + 1) * HALF)
                    return b0[:, cols], HALF, b0h[:, cols], b0l[:, cols]
                cols = slice(G0_START[g], G0_START[g] + G0_WIDTH[g])
                return m0[k * P:(k + 1) * P, cols], G0_WIDTH[g], w0h[:, k, cols], w0l[:, k, cols]

            pool_units = [("A", u, 0) for u in range(LORAS // 4)]
            pool_units += [("B", r, h) for r in range(LORAS * RANK // P) for h in range(2)]
            tables = len(pool_units)
            pool_units += [("W", k, g) for k in range(KC) for g in range(3)]

            def pool_places(n):
                kind, u, v = pool_units[n]
                if kind == "A":
                    src = a1[4 * u:4 * u + 4].rearrange("i p c -> p i c")
                    to = [a1_dram[4 * u:4 * u + 4, :, s * P:(s + 1) * P].rearrange("i p c -> p i c") for s in range(2)]
                elif kind == "B":
                    src = b1[u * P:(u + 1) * P, v * HALF:(v + 1) * HALF]
                    to = [b1_dram[u * P:(u + 1) * P, s, v * HALF:(v + 1) * HALF] for s in range(2)]
                else:
                    cols = slice(G1_AT[v], G1_AT[v] + G1_BASE[v])
                    src = w1t[u * P:(u + 1) * P, G1_COL[v]:G1_COL[v] + G1_BASE[v]]
                    return src, G1_BASE[v], w1h_k[:, u, cols], w1l_k[:, u, cols], None
                cols = slice(n * HALF, (n + 1) * HALF)
                return src, HALF, w1h[:, cols], w1l[:, cols], to

            def pool_pieces(t):
                return range(POOL_PIECES_A_TILE * t, min(POOL_PIECES_A_TILE * (t + 1), len(pool_units)))

            def wq_place(u):
                per = D // WQ_COLS
                return u // per, slice(u % per * WQ_COLS, (u % per + 1) * WQ_COLS)

        with ExitStack() as p2:
            obuf = sb("obuf", [P, 2, D], F32, p2)
            b_stack = [sb(f"b_stack{b}", [STACK, D], F32R, p2) for b in range(2)]
            h_masked = sb("h_masked", [P, LR], F32, p2)
            h_parts = sb("h_parts", [P, 2, LR], F32, p2)
            ht = sb("ht", [STACK, P], F32R, p2)
            val = sb("val", [P, D], F32, p2)
            power = sb("power", [P, D], F32, p2)
            rounded = sb("rounded", [P, D], BF16, p2)
            nan_or_0 = sb("nan_or_0", [P, D], BF16, p2)
            rq = sb("rq", [P, D], BF16, p2)
            rqt = sb("rqt", [P, D], BF16, p2)
            bias2_sb = sb("bias2_sb", [P, D], F32, p2)
            bias_raw = sb("bias_raw", [1, D], F32, p2)
            bias_h = sb("bias_h", [1, D], F32R, p2)
            bias_l = sb("bias_l", [1, D], F32R, p2)

            x1_loaded = [sem(f"x1_loaded{b}") for b in range(2)]
            a_loaded = [sem(f"a_loaded{b}") for b in range(2)]
            b_loaded = [sem(f"b_loaded{b}") for b in range(2)]
            slot_done = sem("slot_done")
            bias2_loaded = sem("bias2_loaded")
            bias_loaded = sem("bias_loaded")
            bias_split = sem("bias_split")
            bias_rows = sem("bias_rows")
            h1_ps = sem("h1_ps")
            turned_loaded = [sem(f"turned_loaded{b}") for b in range(2)]
            main_done = sem("main_done")
            rq_blocks_done = sem("rq_blocks_done")
            masked_done = sem("masked_done")
            h_hi_done = sem("h_hi_done")
            ht_ones = sem("ht_ones")
            h_turned = sem("h_turned")
            h_lo_done = sem("h_lo_done")
            ht_done = [sem(f"ht_done{e}") for e in range(2)]
            r_ps = [sem(f"r_ps{g}") for g in range(3)]
            val_done = [sem(f"val_done{g}") for g in range(3)]
            power_done = sem("power_done")
            scaled_done = sem("scaled_done")
            shifted_done = sem("shifted_done")
            rounded_done = sem("rounded_done")
            nan_done = sem("nan_done")
            rq_done = sem("rq_done")
            rqt_done = [sem(f"rqt_done{e}") for e in range(2)]
            f_ps = [sem(f"f_ps{h}") for h in range(2)]
            x1b_done = sem("x1b_done")
            out_done = [sem(f"out_done{h}") for h in range(2)]
            out_stored = [sem(f"out_stored{b}") for b in range(2)]

            rq_blocks = sb("rq_blocks", [P, D], BF16, p2)

            def turned(operand, h):
                return operand[:, h * HALF:(h + 1) * HALF].rearrange("p (k a j) -> p k a j", k=KC // 2, a=4)

            def in_blocks(tile, h):
                ordered = tile.rearrange("p (a k j) -> p k a j", a=4, k=KC)
                return ordered[:, h * KC // 2:(h + 1) * KC // 2]

            moves = [[(a, q) for a in part for q in range(4)] for part in ((0,), (1, 2, 3))]

            def move_hw(engine_move, share):
                for a, q in moves[share]:
                    last = engine_move(hwt[32 * q:32 * q + 32, :, 32 * a:32 * a + 32],
                                       hw_parts[32 * a:32 * a + 32, :, 32 * q:32 * q + 32])
                last.then_inc(hwt_done[share], 1)

            def move_h(engine_move, share):
                for a in sorted({a for a, _ in moves[share]}):
                    for s, part in enumerate((0, 1, 0)):
                        last = engine_move(ht[LR * s:LR * (s + 1), 32 * a:32 * a + 32],
                                           h_parts[32 * a:32 * a + 32, part, :])
                last.then_inc(ht_done[share], 1)

            last_parts = (range(0, G1_COL[2] // P), range(G1_COL[2] // P, KC))
            rqt_last = xbuf[:, 0, 0:D // 2].bitcast(BF16)

            def blocks_of(tile):
                return tile.rearrange("p (k q j) -> p k q j", q=4, k=KC)

            def move_rq(engine_move, share, to, ks=range(KC)):
                ks = slice(ks.start, ks.stop)
                for a, q in moves[share]:
                    cols = slice(q * D // 4, (q + 1) * D // 4)
                    source = rq_blocks[32 * a:32 * a + 32, cols].rearrange("p (k j) -> p k j", k=KC)
                    rows = to[32 * q:32 * q + 32, :].rearrange("p (k n) -> p k n", k=KC)
                    last = engine_move(rows[:, ks, 32 * a:32 * a + 32], source[:, ks])
                last.then_inc(rqt_done[share], 1)

        with nc.Block() as block:

            @block.sync
            def _(sp):
                sp.dma_start(ids0_sb[:, :], ids0.rearrange("(a n) -> a n", a=1)).then_inc(s_ids, 16)
                sp.dma_start(xbuf[:, 0, :], x_t[0]).then_inc(x_loaded[0], 16)
                sp.wait_ge(s_ids, 16)
                sp.wait_ge(wbd_zeroed, 1)

                def load_cond(t, b):
                    for j in range(PER_TILE):
                        which = sp.value_load(ids0_sb[0:1, bass.ds(PER_TILE * t + j, 1)], min_val=0, max_val=15)
                        rows = slice(j * CH, (j + 1) * CH)
                        sp.dma_start(wbd[rows, b, rows],
                                     wc[bass.ds(which, 1)].rearrange("a c d -> (a c) d")).then_inc(wc_loaded[b], 16)

                load_cond(0, 0)
                for n, unit in enumerate(w0_units):
                    src, width, _, _ = w0_places(unit)
                    if n >= slots:
                        sp.wait_ge(w0_lo, n - slots + 1)
                    sp.dma_start(stage[n % slots][:, 0:width], src).then_inc(stage_loaded[n % slots], 16)
                    if n == KC - 1:
                        sp.dma_start(b_base_sb[:, :], b_base.partition_broadcast(P)).then_inc(b_base_loaded, 16)
                        sp.dma_start(s_in_sb[:, :], s_in.partition_broadcast(P)).then_inc(s_const, 16)
                        sp.dma_start(s_w_sb[:, :], s_w.partition_broadcast(P)).then_inc(s_const, 16)
                        sp.dma_start(xbuf[:, 1, :], x_t[1]).then_inc(x_loaded[1], 16)
                        load_cond(1, 1)
                sp.dma_start(ids1_sb[:, :], ids1.rearrange("(a n) -> a n", a=1)).then_inc(s_ids, 16)

                def load_pool_piece(n):
                    src, width, _, _, _ = pool_places(n)
                    sp.dma_start(raw[:, n % 2, 0:width], src).then_inc(pool_loaded[n % 2], 16)

                def load_wq_piece(u):
                    k, cols = wq_place(u)
                    sp.dma_start(wq_val[:, u % 2, :], wf[k * P:(k + 1) * P, cols])\
                      .then_inc(wq_loaded[u % 2], 16)

                for n in range(2):
                    load_pool_piece(n)
                    load_wq_piece(n)

                def feed(t):
                    quantized = [*wq_pieces(t - 1)[WQ_A_TILE - 1:], *wq_pieces(t)[:WQ_A_TILE - 1]]
                    for n, u in zip_longest(pool_pieces(t), quantized):
                        feed_pool(n)
                        feed_wq(u)

                def feed_pool(n):
                    if n is not None:
                        sp.wait_ge(pool_lo, n + 1)
                        kind = pool_units[n][0]
                        _, _, hi, lo, to = pool_places(n)
                        if to:
                            for dram, part in zip(to, (hi.bitcast(F32), lo.bitcast(F32))):
                                if kind == "A":
                                    part = part.rearrange("p (i c) -> p i c", i=4)
                                sp.dma_start(dram, part).then_inc(split_stored, 16)
                        if n + 2 < len(pool_units):
                            load_pool_piece(n + 2)

                def feed_wq(u):
                    if u is not None and u + 2 < WQ_PIECES:
                        sp.wait_ge(wq_step, WQ_STEPS * (u + 1))
                        load_wq_piece(u + 2)

                def tile(t, b, more):
                    sp.wait_ge(x1_done[2], t + 1)
                    sp.dma_start(x1_dram[bass.ds(t, 1)].rearrange("a p n -> (a p) n"),
                                 x1buf[:, b, :]).then_inc(x1_stored[b], 16)
                    if more:
                        sp.dma_start(xbuf[:, b, :], x_t[bass.ds(t + 2, 1)].rearrange("a p n -> (a p) n"))\
                          .then_inc(x_loaded[b], 16)
                        load_cond(t + 2, b)
                    sp.wait_ge(blocks_done, t + 1)
                    to = x1t_dram[bass.ds(t, 1)].rearrange("o (q i) (a m) -> a (o i) q m", i=32, a=4)
                    for a in range(4):
                        sp.dma_start(to[a], x1_blocks[32 * a:32 * a + 32, :].rearrange("i (q m) -> i q m", q=4))\
                          .then_inc(blocks_stored, 16)

                for t in range(PREP_TILES):
                    feed(t)
                    tile(t, t % 2, True)
                with sp.Fori(PREP_TILES, TILES - 3, 2) as i:
                    tile(i, 0, True)
                    tile(i + 1, 1, True)

                def load_turned(t, b):
                    sp.dma_start(xbuf[:, b, :], x1t_dram[bass.ds(t, 1)].rearrange("a p n -> (a p) n"))\
                      .then_inc(turned_loaded[b], 16)

                def load_x1(t, b):
                    sp.dma_start(x1buf[:, b, :], x1_dram[bass.ds(t, 1)].rearrange("a p n -> (a p) n"))\
                      .then_inc(x1_loaded[b], 16)

                def adapter(row, j):
                    return sp.value_load(ids1_sb[0:1, bass.ds(PER_TILE * row + j, 1)], min_val=0, max_val=LORAS - 1)

                def load_a(which, b, j):
                    sp.dma_start(a_raw[:, b, j, :], a1_dram[bass.ds(which, 1)].rearrange("a p c -> (a p) c"))\
                      .then_inc(a_loaded[b], 16)

                def load_b(which, b, j):
                    for s, part in enumerate((0, 0, 1)):
                        row = s * LR + j * RANK
                        sp.dma_start(b_stack[b][row:row + RANK, :].bitcast(F32),
                                     b1_ids[bass.ds(which, 1), :, part, :].rearrange("a r n -> (a r) n"))\
                          .then_inc(b_loaded[b], 16)

                sp.wait_ge(s_ids, 32)
                sp.wait_ge(split_stored, 32 * tables)
                sp.wait_ge(pool_lo, len(pool_units))
                for t in range(2):
                    for j in range(PER_TILE):
                        load_a(adapter(t, j), t, j)
                tile(TILES - 2, 0, False)
                sp.wait_ge(x1_stored[0], 16 * (TILES // 2))
                sp.wait_ge(blocks_stored, 64 * (TILES - 1))
                load_turned(0, 0)
                load_x1(0, 0)
                tile(TILES - 1, 1, False)
                sp.dma_start(bias_raw[:, :], base_bias.rearrange("(a n) -> a n", a=1)).then_inc(bias_loaded, 16)
                load_turned(1, 1)
                for j in range(PER_TILE):
                    load_b(adapter(0, j), 0, j)
                sp.wait_ge(x1_stored[1], 16 * (TILES // 2))
                sp.wait_ge(blocks_stored, 64 * TILES)
                sp.dma_start(bias2_sb[:, :], bias2.partition_broadcast(P)).then_inc(bias2_loaded, 16)
                load_x1(1, 1)
                sp.wait_ge(bias_split, 2)
                for b in range(2):
                    for s, part in enumerate((bias_h, bias_l)):
                        sp.dma_start(b_stack[b][3 * LR + s:3 * LR + s + 1, :].bitcast(F32),
                                     part[:, :].bitcast(F32)).then_inc(bias_rows, 16)

                def store_out(t, b):
                    sp.wait_ge(out_done[1], t + 1)
                    sp.dma_start(out_t[bass.ds(t, 1)].rearrange("a p n -> (a p) n"), obuf[:, b, :])\
                      .then_inc(out_stored[b], 16)

                def tile(t, b, first, lag, more):
                    if more >= 1:
                        if not first:
                            sp.wait_ge(r_ps[2], t)
                            sp.wait_ge(slot_done, t)
                        for j in range(PER_TILE):
                            which = adapter(t + 1, j)
                            if not first:
                                load_a(which, 1 - b, j)
                            load_b(which, 1 - b, j)
                    if lag:
                        store_out(t - 2, b)
                    if more == 2:
                        sp.wait_ge(lo_done[1], TILES + t + 1)
                        sp.wait_ge(x1b_done, t + 1)
                        load_turned(t + 2, b)
                        load_x1(t + 2, b)

                tile(0, 0, True, False, 2)
                tile(1, 1, False, False, 2)
                with sp.Fori(2, TILES - 3, 2) as i:
                    tile(i, 0, False, True, 2)
                    tile(i + 1, 1, False, True, 2)
                tile(TILES - 2, 0, False, True, 1)
                tile(TILES - 1, 1, False, True, 0)
                store_out(TILES - 2, 0)
                store_out(TILES - 1, 1)
                for b in range(2):
                    sp.wait_ge(out_stored[b], 16 * TILES // 2)

            @block.gpsimd
            def _(pool):
                pool.memset(wbd[:, :, :], 0.0).then_inc(wbd_zeroed, 1)
                pool.memset(ones[:, :], 1.0).then_inc(ones_set, 1)
                pool.wait_ge(b_base_loaded, 16)

                def add_bias(t, b):
                    pool.wait_ge(st_ps[1], t + 1)
                    pool.tensor_tensor(xbuf[:, b, :], xbuf[:, b, :], b_base_sb[:, :], ALU.add).then_inc(xb_done, 1)

                def split(n):
                    _, width, hi, lo, _ = pool_places(n)
                    piece = raw[:, n % 2, 0:width]
                    pool.wait_ge(pool_loaded[n % 2], 16 * (n // 2 + 1))
                    if n == tables:
                        pool.wait_ge(split_stored, 32 * tables)
                    pool.tensor_scalar(hi, piece, 1.0, None, ALU.mult).then_inc(pool_hi, 1)
                    pool.wait_ge(pool_hi, n + 1)
                    pool.tensor_tensor(lo, piece, hi, ALU.subtract).then_inc(pool_lo, 1)

                for t in range(PREP_TILES):
                    add_bias(t, t % 2)
                    for n in pool_pieces(t):
                        split(n)
                with pool.Fori(PREP_TILES, TILES - 1, 2) as i:
                    add_bias(i, 0)
                    add_bias(i + 1, 1)

                one = ones[:, :].unsqueeze(2)

                def fill_slot(t, b, loads):
                    pool.wait_ge(a_loaded[b], 32 * loads)
                    if not (isinstance(t, int) and t == 0):
                        pool.wait_ge(h1_ps, t)
                    for s, w in enumerate((w1h_k, w1l_k)):
                        to = w[:, :, 0:LR].rearrange("p k (j r) -> p j k r", j=PER_TILE)
                        for j in range(PER_TILE):
                            part = a_raw[:, b, j, s * P:(s + 1) * P].rearrange("p (k r) -> p k r", r=RANK)
                            last = pool.tensor_tensor(to[:, j], part, one.to_broadcast([P, KC, RANK]), ALU.mult)
                    last.then_inc(slot_done, 1)

                pool.wait_ge(ones_set, 1)
                fill_slot(0, 0, 1)
                pool.wait_ge(x1_done[2], TILES)
                pool.wait_ge(bias2_loaded, 16)

                def tile(t, b, x1_loads, a_loads, stored):
                    if a_loads is not None:
                        fill_slot(t + 1, 1 - b, a_loads)
                    pool.wait_ge(x1_loaded[b], 16 * x1_loads)
                    if stored is not None:
                        pool.wait_ge(out_stored[b], stored)
                    pool.tensor_tensor(obuf[:, b, :], x1buf[:, b, :], bias2_sb[:, :], ALU.add).then_inc(x1b_done, 1)

                tile(0, 0, 1, 1, None)
                tile(1, 1, 1, 2, None)
                with pool.Fori(2, TILES - 3, 2) as i:
                    half = pool.snap(i // 2)
                    tile(i, 0, half + 1, half + 1, 8 * i)
                    tile(i + 1, 1, half + 1, half + 2, 8 * i)
                tile(TILES - 2, 0, TILES // 2, TILES // 2, 8 * (TILES - 2))
                tile(TILES - 1, 1, TILES // 2, None, 8 * (TILES - 2))

            @block.scalar
            def _(act):
                def copy(to, source):
                    return act.activation(to, source, ACT.Copy)

                def st_hi(t):
                    for h in range(2):
                        act.wait_ge(st_ps[h], t + 1)
                        act.activation(st_h[:, h * HALF:(h + 1) * HALF], bank_t[:, h, :], ACT.Copy)\
                           .then_inc(hi_done[h], 1)

                for n, unit in enumerate(w0_units):
                    _, width, hi, _ = w0_places(unit)
                    act.wait_ge(stage_loaded[n % slots], 16 * (n // slots + 1))
                    act.activation(hi, stage[n % slots][:, 0:width], ACT.Copy,
                                   scale=LORA_SCALE if unit[0] == "b" else 1.0).then_inc(w0_hi, 1)
                    if n == 1:
                        st_hi(0)

                def tile(t, more):
                    act.wait_ge(negmax_done, t + 1)
                    act.activation(expo[:, :], bank_g[:, 0, ER:ER + EXPERTS], ACT.Exp, bias=negmax[:, :],
                                   accum_out=esum[:, :]).then_inc(exp_done, 1)
                    act.wait_ge(hw_lo_done, t + 1)
                    move_hw(copy, 0)
                    if more:
                        st_hi(t + 1)

                tile(0, True)
                tile(1, True)
                with act.Fori(2, TILES - 3, 2) as i:
                    tile(i, True)
                    tile(i + 1, True)
                tile(TILES - 2, True)
                tile(TILES - 1, False)

                def turned_hi(t, b, loads):
                    act.wait_ge(turned_loaded[b], 16 * loads)
                    act.wait_ge(main_done, t + 1)
                    for h in range(2):
                        act.activation(turned(st_h[:, :], h), in_blocks(xbuf[:, b, :], h), ACT.Copy)\
                           .then_inc(hi_done[h], 1)

                turned_hi(0, 0, 1)
                act.wait_ge(x1_done[2], TILES)
                act.wait_ge(bias_loaded, 16)
                act.activation(bias_h[:, :], bias_raw[:, :], ACT.Copy).then_inc(bias_split, 1)

                def turn_rq(t):
                    act.wait_ge(rq_blocks_done, t + 1)
                    move_rq(copy, 0, rqt[:, :])

                def tile(t, b, lag, loads):
                    act.wait_ge(h_lo_done, t + 1)
                    move_h(copy, 0)
                    if lag:
                        turn_rq(t - 1)
                    if loads is not None:
                        turned_hi(t + 1, 1 - b, loads)
                    if lag:
                        act.wait_ge(rounded_done, t)
                    for g in range(3):
                        act.wait_ge(r_ps[g], t + 1)
                        at = LR if g == 0 else 0
                        act.activation(val[:, G1_COL[g]:G1_COL[g] + G1_BASE[g]],
                                       bank_g[:, g, at:at + G1_BASE[g]], ACT.Copy, scale=inv_in[:, :])\
                           .then_inc(val_done[g], 1)

                tile(0, 0, False, 1)
                tile(1, 1, True, 2)
                with act.Fori(2, TILES - 3, 2) as i:
                    half = act.snap(i // 2)
                    tile(i, 0, True, half + 1)
                    tile(i + 1, 1, True, half + 2)
                tile(TILES - 2, 0, True, TILES // 2)
                tile(TILES - 1, 1, True, None)
                for n, ks in enumerate(last_parts):
                    act.wait_ge(rq_blocks_done, TILES + n)
                    move_rq(copy, 0, rqt_last, ks)

            @block.vector
            def _(dve):
                dve.memset(probs[:, :], -1.0).then_inc(probs_done, 1)
                dve.memset(to_replace[:, :], -1.0).then_inc(replace_done, 1)
                dve.memset(slot_mask[:, :], 0.0).then_inc(mask_set, 1)
                dve.wait_ge(mask_set, 1)
                for j in range(PER_TILE):
                    dve.memset(slot_mask[j * CH:(j + 1) * CH, j * RANK:(j + 1) * RANK], 1.0).then_inc(mask_set, 1)

                def st_lo(t, h):
                    half = slice(h * HALF, (h + 1) * HALF)
                    dve.wait_ge(hi_done[h], t + 1)
                    dve.tensor_tensor(st_l[:, half], bank_t[:, h, :], st_h[:, half], ALU.subtract)\
                       .then_inc(lo_done[h], 1)

                for n, unit in enumerate(w0_units):
                    _, width, hi, lo = w0_places(unit)
                    dve.wait_ge(w0_hi, n + 1)
                    piece = stage[n % slots][:, 0:width]
                    if unit[0] == "b":
                        dve.scalar_tensor_tensor(lo, piece, LORA_SCALE, hi, ALU.mult, ALU.subtract).then_inc(w0_lo, 1)
                    else:
                        dve.tensor_tensor(lo, piece, hi, ALU.subtract).then_inc(w0_lo, 1)
                    if n == 1:
                        st_lo(0, 0)
                        st_lo(0, 1)
                dve.wait_ge(s_const, 32)
                dve.reciprocal(inv_in[:, :], s_in_sb[:, :]).then_inc(s_scale, 1)
                dve.reciprocal(inv_w[:, :], s_w_sb[:, :]).then_inc(s_scale, 1)
                dve.tensor_tensor(s_out[:, :], s_in_sb[:, :], s_w_sb[:, :], ALU.mult).then_inc(s_scale, 1)
                dve.wait_ge(s_scale, 3)

                def quantize_weight(u):
                    val = wq_val[:, u % 2, :]
                    power = wq_pow[:, :]
                    k, cols = wq_place(u)
                    to = wq[:, k, cols]
                    base = WQ_STEPS * u
                    dve.wait_ge(wq_loaded[u % 2], 16 * (u // 2 + 1))
                    dve.tensor_scalar(val, val, inv_w[:, :], None, ALU.mult).then_inc(wq_step, 1)
                    dve.wait_ge(wq_step, base + 1)
                    dve.tensor_scalar(power.bitcast(U32), val.bitcast(U32), 0x7F800000, None, ALU.bitwise_and)\
                       .then_inc(wq_step, 1)
                    dve.wait_ge(wq_step, base + 2)
                    dve.tensor_scalar(power, power, MIN_NORMAL, ROUND_C, ALU.max, ALU.mult).then_inc(wq_step, 1)
                    dve.wait_ge(wq_step, base + 3)
                    dve.tensor_tensor(val, val, power, ALU.add).then_inc(wq_step, 1)
                    dve.wait_ge(wq_step, base + 4)
                    dve.tensor_tensor(to, val, power, ALU.subtract).then_inc(wq_step, 1)
                    dve.wait_ge(wq_step, base + 5)
                    dve.tensor_scalar(wq_nan, to, OVERFLOW_C, 0.0, ALU.mult, ALU.mult).then_inc(wq_step, 1)
                    dve.wait_ge(wq_step, base + 6)
                    dve.tensor_tensor(to, to, wq_nan, ALU.add).then_inc(wq_step, 1)

                def tile(t, b, stored, blocks, more, wq_units=()):
                    n = t + 1
                    dve.wait_ge(h_ps, n)
                    dve.tensor_reduce(negmax[:, :], bank_g[:, 0, ER:ER + EXPERTS], AXIS.X, ALU.max, negate=True)\
                       .then_inc(negmax_done, 1)
                    dve.wait_ge(exp_done, n)
                    dve.reciprocal(rsum[:, :], esum[:, :]).then_inc(rsum_done, 1)
                    dve.max(sorted8[:, :], expo[:, :]).then_inc(sorted_done, 1)
                    dve.wait_ge(rsum_done, n)
                    dve.tensor_scalar(probs[:, 0:EXPERTS], expo[:, :], rsum[:, :], None, ALU.mult)\
                       .then_inc(probs_done, 1)
                    dve.wait_ge(sorted_done, n)
                    dve.tensor_scalar(to_replace[:, 0:2], sorted8[:, 0:2], rsum[:, :], None, ALU.mult)\
                       .then_inc(replace_done, 1)
                    dve.wait_ge(probs_done, n + 1)
                    dve.wait_ge(replace_done, n + 1)
                    dve.tensor_tensor(top_sum[:, :], to_replace[:, 0:1], to_replace[:, 1:2], ALU.add)\
                       .then_inc(top_sum_done, 1)
                    dve.match_replace(without_top[:, :], to_replace[:, :], probs[:, :], 0.0)\
                       .then_inc(without_done, 1)
                    dve.wait_ge(top_sum_done, n)
                    dve.reciprocal(top_inv[:, :], top_sum[:, :]).then_inc(top_inv_done, 1)
                    dve.wait_ge(without_done, n)
                    dve.tensor_tensor(top_probs[:, :], probs[:, 0:EXPERTS], without_top[:, 0:EXPERTS],
                                      ALU.subtract).then_inc(top_done, 1)
                    dve.wait_ge(top_done, n)
                    dve.wait_ge(top_inv_done, n)
                    gate = top_probs[:, :].unsqueeze(2).to_broadcast([P, EXPERTS, RANK])
                    dve.scalar_tensor_tensor(hw[:, :].rearrange("p (e r) -> p e r", r=RANK),
                                             bank_g[:, 0, 0:ER].rearrange("p (e r) -> p e r", r=RANK),
                                             top_inv[:, :], gate, ALU.mult, ALU.mult).then_inc(hw_done, 1)
                    hi, lo = hw_parts[:, 0, :], hw_parts[:, 1, :]
                    dve.wait_ge(hw_done, n)
                    dve.transpose(lo, hw[:, :]).then_inc(hw_turned, 1)
                    dve.wait_ge(hw_turned, n)
                    dve.tensor_copy(hi.bitcast(F32R), lo).then_inc(hw_hi_done, 1)
                    dve.wait_ge(hw_hi_done, n)
                    dve.tensor_tensor(lo, lo, hi, ALU.subtract).then_inc(hw_lo_done, 1)
                    dve.wait_ge(hw_lo_done, n)
                    move_hw(dve.tensor_copy, 1)
                    for u in wq_units[0:1]:
                        quantize_weight(u)
                    for u in wq_units[1:WQ_A_TILE - 1]:
                        quantize_weight(u)
                    if more:
                        st_lo(n, 0)
                    dve.wait_ge(xb_done, n)
                    if stored is not None:
                        dve.wait_ge(x1_stored[b], stored)
                    for g in range(3):
                        dve.wait_ge(acc_ps[g], n)
                        width = G0_WIDTH[g] - G0_OUT[g]
                        cols = slice(G0_COL[g], G0_COL[g] + width)
                        dve.tensor_tensor(x1buf[:, b, cols], bank_g[:, g, G0_OUT[g]:G0_WIDTH[g]],
                                          xbuf[:, b, cols], ALU.add).then_inc(x1_done[g], 1)
                        if g == 0 and more:
                            st_lo(n, 1)
                    dve.wait_ge(x1_done[2], n)
                    if blocks is not None:
                        dve.wait_ge(blocks_stored, blocks)
                    dve.transpose(x1_blocks[:, :].rearrange("p (q k j) -> p k q j", q=4, k=KC),
                                  x1buf[:, b, :].rearrange("p (k q j) -> p k q j", q=4, k=KC)).then_inc(blocks_done, 1)
                    for u in wq_units[WQ_A_TILE - 1:]:
                        quantize_weight(u)

                for t in range(PREP_TILES):
                    tile(t, t % 2, 16 * (t // 2) if t >= 2 else None, 64 * t if t else None, True, wq_pieces(t))
                with dve.Fori(PREP_TILES, TILES - 3, 2) as i:
                    tile(i, 0, 8 * i, 64 * i, True)
                    tile(i + 1, 1, 8 * i, 64 * (i + 1), True)
                tile(TILES - 2, 0, 8 * (TILES - 2), 64 * (TILES - 2), True)
                tile(TILES - 1, 1, 8 * (TILES - 2), 64 * (TILES - 1), False)

                def quantize(n, tiles, cols=slice(0, D), g=2):
                    v, w = val[:, cols], power[:, cols]
                    dve.wait_ge(val_done[g], tiles)
                    dve.tensor_scalar(w.bitcast(U32), v.bitcast(U32), 0x7F800000, None,
                                      ALU.bitwise_and).then_inc(power_done, 1)
                    dve.wait_ge(power_done, n)
                    dve.tensor_scalar(w, w, MIN_NORMAL, ROUND_C, ALU.max, ALU.mult).then_inc(scaled_done, 1)
                    dve.wait_ge(scaled_done, n)
                    dve.tensor_tensor(v, v, w, ALU.add).then_inc(shifted_done, 1)
                    dve.wait_ge(shifted_done, n)
                    dve.tensor_tensor(rounded[:, cols], v, w, ALU.subtract).then_inc(rounded_done, 1)
                    dve.wait_ge(rounded_done, n)
                    dve.tensor_scalar(nan_or_0[:, cols], rounded[:, cols], OVERFLOW_C, 0.0, ALU.mult, ALU.mult)\
                       .then_inc(nan_done, 1)
                    dve.wait_ge(nan_done, n)
                    dve.tensor_tensor(rq[:, cols], rounded[:, cols], nan_or_0[:, cols], ALU.add)\
                       .then_inc(rq_done, 1)

                def turn_rq(n, to, ks=range(KC)):
                    part = slice(ks.start, ks.stop)
                    dve.wait_ge(rq_done, n)
                    dve.transpose(rq_blocks[:, :].rearrange("p (q k j) -> p k q j", q=4, k=KC)[:, part],
                                  blocks_of(rq[:, :])[:, part]).then_inc(rq_blocks_done, 1)
                    dve.wait_ge(rq_blocks_done, n)
                    move_rq(dve.tensor_copy, 1, to, ks)

                def turned_lo(t, b):
                    for h in range(2):
                        dve.wait_ge(hi_done[h], TILES + t + 1)
                        last = dve.tensor_tensor(turned(st_l[:, :], h), in_blocks(xbuf[:, b, :], h),
                                                 turned(st_h[:, :], h), ALU.subtract)
                        last.then_inc(lo_done[h], 1)

                def finish(t, b, bank=bank_f):
                    dve.wait_ge(x1b_done, t + 1)
                    for h in range(2):
                        half = slice(h * HALF, (h + 1) * HALF)
                        dve.wait_ge(f_ps[h], t + 1)
                        dve.scalar_tensor_tensor(obuf[:, b, half], bank[:, h, :], s_out[:, :],
                                                 obuf[:, b, half], ALU.mult, ALU.add).then_inc(out_done[h], 1)

                def stack_h(t):
                    n = t + 1
                    dve.wait_ge(h1_ps, n)
                    dve.tensor_tensor(h_masked[:, :], bank_g[:, 0, 0:LR], slot_mask[:, :], ALU.mult)\
                       .then_inc(masked_done, 1)
                    dve.wait_ge(masked_done, n)
                    hi, lo = h_parts[:, 0, :], h_parts[:, 1, :]
                    dve.transpose(lo, h_masked[:, :]).then_inc(h_turned, 1)
                    dve.wait_ge(h_turned, n)
                    dve.tensor_copy(hi.bitcast(F32R), lo).then_inc(h_hi_done, 1)
                    dve.wait_ge(h_hi_done, n)
                    dve.tensor_tensor(lo, lo, hi, ALU.subtract).then_inc(h_lo_done, 1)
                    dve.wait_ge(h_lo_done, n)
                    move_h(dve.tensor_copy, 1)

                def tile(t, b, lag, more):
                    if lag >= 1:
                        quantize(t, t)
                    stack_h(t)
                    if lag >= 1:
                        turn_rq(t, rqt[:, :])
                    if lag >= 2:
                        finish(t - 2, b)
                    if more:
                        turned_lo(t + 1, 1 - b)

                turned_lo(0, 0)
                dve.wait_ge(ones_set, 1)
                dve.tensor_copy(ht[3 * LR:STACK, :], ones[3 * LR:STACK, :].to_broadcast([2, P])).then_inc(ht_ones, 1)
                dve.wait_ge(bias_split, 1)
                dve.tensor_tensor(bias_l[:, :], bias_raw[:, :], bias_h[:, :], ALU.subtract).then_inc(bias_split, 1)
                tile(0, 0, 0, True)
                tile(1, 1, 1, True)
                with dve.Fori(2, TILES - 3, 2) as i:
                    tile(i, 0, 2, True)
                    tile(i + 1, 1, 2, True)
                tile(TILES - 2, 0, 2, True)
                tile(TILES - 1, 1, 2, False)
                for n, ks in enumerate(last_parts):
                    quantize(TILES + n, TILES, slice(ks.start * P, ks.stop * P), n + 1)
                    turn_rq(TILES + n, rqt_last, ks)
                finish(TILES - 2, 0)
                finish(TILES - 1, 1, bank_t)

            @block.tensor
            def _(pe):
                def cond(t, b, loads):
                    pe.wait_ge(x_loaded[b], 16 * loads)
                    pe.wait_ge(wc_loaded[b], 32 * loads)
                    for k in range(KC):
                        cols = slice((k % 4) * P, (k % 4 + 1) * P)
                        last = pe.matmul(bank_t[:, k // 4, cols], xbuf[:, b, k * P:(k + 1) * P], wbd[:, b, :],
                                         start=True, stop=True)
                        if k % 4 == 3:
                            last.then_inc(st_ps[k // 4], 1)

                def bank(g, n, split=True):
                    cols = slice(G0_START[g], G0_START[g] + G0_WIDTH[g])
                    to = bank_g[:, g, 0:G0_WIDTH[g]]
                    for k in range(KC):
                        if g == 0 and k == KC // 2:
                            pe.wait_ge(lo_done[1], n)
                        if not split:
                            pe.wait_ge(w0_lo, w0_need[g] - KC + k + 1)
                        rows = slice(k * P, (k + 1) * P)
                        pe.matmul(to, st_h[:, rows], w0h[:, k, cols], start=(k == 0), stop=False)
                        pe.matmul(to, st_h[:, rows], w0l[:, k, cols], start=False, stop=False)
                        last = pe.matmul(to, st_l[:, rows], w0h[:, k, cols], start=False, stop=(k == KC - 1))
                    return last

                def tile(t, b, loads, prior, more):
                    n = t + 1
                    pe.wait_ge(lo_done[0], n)
                    for g in range(3):
                        if prior:
                            pe.wait_ge(x1_done[g], t)
                        last = bank(g, n, prior)
                        if g == 0:
                            last.then_inc(h_ps, 1)
                        if g == 2 and not more:
                            last.then_inc(main_done, 1)
                    if more:
                        cond(n, 1 - b, loads)
                    for e in range(2):
                        pe.wait_ge(hwt_done[e], n)
                    for g in range(3):
                        to = bank_g[:, g, G0_OUT[g]:G0_WIDTH[g]]
                        cols = slice(G0_COL[g], G0_COL[g] + G0_WIDTH[g] - G0_OUT[g])
                        pe.matmul(to, hwt[:, 0, :], b0h[:, cols], start=False, stop=False, skip_group_check=True)
                        pe.matmul(to, hwt[:, 0, :], b0l[:, cols], start=False, stop=False, skip_group_check=True)
                        pe.matmul(to, hwt[:, 1, :], b0h[:, cols], start=False, stop=True, skip_group_check=True)\
                          .then_inc(acc_ps[g], 1)

                cond(0, 0, 1)
                tile(0, 0, 1, False, True)
                tile(1, 1, 2, True, True)
                with pe.Fori(2, TILES - 3, 2) as i:
                    half = pe.snap(i // 2)
                    tile(i, 0, half + 1, True, True)
                    tile(i + 1, 1, half + 2, True, True)
                tile(TILES - 2, 0, TILES // 2, True, True)
                tile(TILES - 1, 1, None, True, False)

                def bank(g, n):
                    cols = slice(G1_AT[g] - (LR if g == 0 else 0), G1_AT[g] + G1_BASE[g])
                    to = bank_g[:, g, 0:cols.stop - cols.start]
                    for k in range(KC):
                        if g == 0 and k == KC // 2:
                            pe.wait_ge(lo_done[1], TILES + n)
                        rows = slice(k * P, (k + 1) * P)
                        pe.matmul(to, st_h[:, rows], w1h_k[:, k, cols], start=(k == 0), stop=False)
                        pe.matmul(to, st_h[:, rows], w1l_k[:, k, cols], start=False, stop=False)
                        last = pe.matmul(to, st_l[:, rows], w1h_k[:, k, cols], start=False, stop=(k == KC - 1))
                    return last

                def ffn(t):
                    for e in range(2):
                        pe.wait_ge(rqt_done[e], t + 1)
                    for h in range(2):
                        for k in range(KC):
                            last = pe.matmul(bank_f[:, h, :], rqt[:, k * P:(k + 1) * P],
                                             wq[:, k, h * HALF:(h + 1) * HALF], start=(k == 0), stop=(k == KC - 1))
                        last.then_inc(f_ps[h], 1)

                def last_ffn():
                    for n, ks in enumerate(last_parts):
                        for e in range(2):
                            pe.wait_ge(rqt_done[e], TILES + n)
                        for h in range(2):
                            for k in ks:
                                last = pe.matmul(bank_t[:, h, :], rqt_last[:, k * P:(k + 1) * P],
                                                 wq[:, k, h * HALF:(h + 1) * HALF],
                                                 start=(k == 0), stop=(k == KC - 1))
                            if n == 1:
                                last.then_inc(f_ps[h], 1)

                def main(t, g, lag):
                    if lag:
                        pe.wait_ge(val_done[g], t)
                    else:
                        pe.wait_ge(x1_done[g], TILES)
                    last = bank(g, t + 1)
                    if g == 0:
                        last.then_inc(h1_ps, 1)
                    if g == 2:
                        last.then_inc(main_done, 1)

                def stacks_in(t, b, loads):
                    pe.wait_ge(b_loaded[b], 96 * loads)
                    for e in range(2):
                        pe.wait_ge(ht_done[e], t + 1)

                def add_lora(g, b):
                    at = LR if g == 0 else 0
                    pe.matmul(bank_g[:, g, at:at + G1_BASE[g]], ht[:, :],
                              b_stack[b][:, G1_COL[g]:G1_COL[g] + G1_BASE[g]],
                              start=False, stop=True, skip_group_check=True).then_inc(r_ps[g], 1)

                def operands_in(t):
                    pe.wait_ge(lo_done[0], TILES + t + 1)
                    pe.wait_ge(slot_done, t + 1)

                def tile(t, b, loads, lag):
                    operands_in(t)
                    for g in range(3):
                        main(t, g, lag)
                    if not lag:
                        pe.wait_ge(bias_rows, 64)
                        pe.wait_ge(ht_ones, 1)
                    stacks_in(t, b, loads)
                    for g in range(3):
                        add_lora(g, b)
                    if lag == 2:
                        pe.wait_ge(out_done[1], t - 1)
                    if lag:
                        ffn(t - 1)

                tile(0, 0, 1, 0)
                tile(1, 1, 1, 1)
                with pe.Fori(2, TILES - 3, 2) as i:
                    half = pe.snap(i // 2)
                    tile(i, 0, half + 1, 2)
                    tile(i + 1, 1, half + 1, 2)
                tile(TILES - 2, 0, TILES // 2, 2)
                operands_in(TILES - 1)
                main(TILES - 1, 0, 2)
                main(TILES - 1, 1, 2)
                stacks_in(TILES - 1, 1, TILES // 2)
                add_lora(0, 1)
                add_lora(1, 1)
                main(TILES - 1, 2, 2)
                add_lora(2, 1)
                pe.wait_ge(out_done[1], TILES - 2)
                ffn(TILES - 2)
                last_ffn()


def kernel(x, itok_B_0_15, itok_B_6_15, L0_cond_weights, L0_ffn_W_base, L0_ffn_b_base, L0_ffn_W_router,
           L0_ffn_A, L0_ffn_B, L1_cond_base_weight, L1_cond_base_bias, L1_cond_lora_A_w, L1_cond_lora_B_w,
           L1_ffn_weight, L1_ffn_bias, L1_ffn_input_scale, L1_ffn_weight_scale):
    import concourse.bacc as bacc
    from concourse.bass_utils import run_bass_kernel_spmd

    def lay(a):
        return np.ascontiguousarray(a)

    a_w = np.asarray(L1_cond_lora_A_w)
    arrays = {
        "x": lay(x),
        "ids0": lay(itok_B_0_15),
        "ids1": lay(itok_B_6_15),
        "wc": lay(L0_cond_weights),
        "m0": lay(np.concatenate([np.asarray(L0_ffn_A).reshape(ER, D), np.asarray(L0_ffn_W_router),
                                  np.asarray(L0_ffn_W_base)]).T),
        "b0": lay(np.asarray(L0_ffn_B).transpose(0, 2, 1).reshape(ER, D)),
        "b_base": lay(L0_ffn_b_base),
        "w1t": lay(np.asarray(L1_cond_base_weight).T),
        "base_bias": lay(L1_cond_base_bias),
        "a1": lay(a_w.reshape(LORAS, RANK, KC, P).transpose(0, 3, 2, 1).reshape(LORAS, P, KC * RANK)),
        "b1": lay(np.asarray(L1_cond_lora_B_w).transpose(0, 2, 1).reshape(LORAS * RANK, D)),
        "wf": lay(L1_ffn_weight),
        "bias2": lay(L1_ffn_bias),
        "s_in": lay(L1_ffn_input_scale),
        "s_w": lay(L1_ffn_weight_scale),
    }
    nc = bacc.Bacc("TRN2", target_bir_lowering=False, num_devices=1)
    args = {n: nc.dram_tensor(n, a.shape, mybir.dt.from_np(a.dtype), kind="ExternalInput").ap()
            for n, a in arrays.items()}
    out = nc.dram_tensor("out", (BATCH, CH, D), F32, kind="ExternalOutput").ap()
    build(nc, out=out, **args)
    r = run_bass_kernel_spmd(nc, [arrays], core_ids=[0])
    return r.results[0]["out"]
```
